# Optimizing a Trainium2 kernel written in Bass

```python
import numpy as np
import jax
import jax.numpy as jnp

def _softmax(x, axis=-1):
    return jax.nn.softmax(x, axis=axis)

def _gelu(x):
    return jax.nn.gelu(x, approximate=True)

def _silu(x):
    return jax.nn.silu(x)

def _sigmoid(x):
    return jax.nn.sigmoid(x)

def _layernorm(x, axis=-1, eps=1e-05):
    m = jnp.mean(x, axis=axis, keepdims=True)
    v = jnp.var(x, axis=axis, keepdims=True)
    return (x - m) / jnp.sqrt(v + eps)

def _scatter_add(tgt, idx, src, axis=0):
    return tgt.at[idx].add(src)

def _segment_sum(src, seg, n):
    return jax.ops.segment_sum(src, seg, n)
kernel_name = 'mk_prb_d1_jaxref_r8_723270'

def setup_inputs(seed: int=0):
    np.random.seed(seed)
    _w = jnp.asarray

    def _L0_attn_setup():
        import jax, jax.numpy as jnp
        import numpy as np
        B, N, E = (4, 512, 256)
        H_DIM = 256
        HEADS = 16
        DH = H_DIM // HEADS
        LN_EPS = 1e-05

        def _heads(t):
            b, n, _ = t.shape
            return t.reshape(b, n, HEADS, DH).transpose(0, 2, 1, 3)

        def _layernorm(x, g, b):
            mu = jnp.mean(x, axis=-1, keepdims=True)
            var = jnp.mean(jnp.square(x - mu), axis=-1, keepdims=True)
            return (x - mu) * jax.lax.rsqrt(var + LN_EPS) * g + b
        key = jax.random.key(seed)
        ks = jax.random.split(key, 10)
        s = 1.0 / np.sqrt(E)
        so = 1.0 / np.sqrt(H_DIM)
        return {'x': jax.random.normal(ks[0], (B, N, E), jnp.float32), 'Wqk': jax.random.normal(ks[1], (E, H_DIM), jnp.float32) * s, 'bqk': jnp.zeros((H_DIM,), jnp.float32), 'Wv': jax.random.normal(ks[2], (E, H_DIM), jnp.float32) * s, 'bv': jnp.zeros((H_DIM,), jnp.float32), 'Wu': jax.random.normal(ks[3], (E, H_DIM), jnp.float32) * s, 'bu': jnp.zeros((H_DIM,), jnp.float32), 'Wo': jax.random.normal(ks[4], (H_DIM, E), jnp.float32) * so, 'bo': jnp.zeros((E,), jnp.float32), 'ln_g': jnp.ones((H_DIM,), jnp.float32), 'ln_b': jnp.zeros((H_DIM,), jnp.float32)}
    _L0_attn_in = _L0_attn_setup()

    def _L0_ffn_setup():
        import jax, jax.numpy as jnp
        import numpy as np
        NUM_ACT = 2
        key = jax.random.key(seed)
        k1, k2, k3, k4, k5 = jax.random.split(key, 5)
        B, S, D, I, E = (4, 64, 256, 512, 8)
        x = jax.random.normal(k1, (B, S, D), dtype=jnp.float32)
        gate_w = jax.random.normal(k2, (E, D), dtype=jnp.float32) * 0.02
        w1 = jax.random.normal(k3, (E, I, D), dtype=jnp.float32) * 0.02
        w2 = jax.random.normal(k4, (E, D, I), dtype=jnp.float32) * 0.02
        w3 = jax.random.normal(k5, (E, I, D), dtype=jnp.float32) * 0.02
        return {'x': x, 'gate_w': gate_w, 'w1': w1, 'w2': w2, 'w3': w3}
    _L0_ffn_in = _L0_ffn_setup()
    _d = {'L0_attn_x': _L0_attn_in['x'], 'L0_attn_Wqk': _L0_attn_in['Wqk'], 'L0_attn_bqk': _L0_attn_in['bqk'], 'L0_attn_Wv': _L0_attn_in['Wv'], 'L0_attn_bv': _L0_attn_in['bv'], 'L0_attn_Wu': _L0_attn_in['Wu'], 'L0_attn_bu': _L0_attn_in['bu'], 'L0_attn_Wo': _L0_attn_in['Wo'], 'L0_attn_bo': _L0_attn_in['bo'], 'L0_attn_ln_g': _L0_attn_in['ln_g'], 'L0_attn_ln_b': _L0_attn_in['ln_b'], 'L0_ffn_gate_w': _L0_ffn_in['gate_w'], 'L0_ffn_w1': _L0_ffn_in['w1'], 'L0_ffn_w2': _L0_ffn_in['w2'], 'L0_ffn_w3': _L0_ffn_in['w3']}
    _x0 = _d['L0_attn_x']
    _d['L0_attn_x'] = jax.random.normal(jax.random.fold_in(jax.random.key(seed), 1), (2, 1024, 256), dtype=_x0.dtype)
    del _x0
    return _d

def reference(L0_attn_x, L0_attn_Wqk, L0_attn_bqk, L0_attn_Wv, L0_attn_bv, L0_attn_Wu, L0_attn_bu, L0_attn_Wo, L0_attn_bo, L0_attn_ln_g, L0_attn_ln_b, L0_ffn_gate_w, L0_ffn_w1, L0_ffn_w2, L0_ffn_w3):

    def _L0_attn_ref(x, Wqk, bqk, Wv, bv, Wu, bu, Wo, bo, ln_g, ln_b):
        import jax, jax.numpy as jnp
        import numpy as np
        B, N, E = (4, 512, 256)
        H_DIM = 256
        HEADS = 16
        DH = H_DIM // HEADS
        LN_EPS = 1e-05

        def _heads(t):
            b, n, _ = t.shape
            return t.reshape(b, n, HEADS, DH).transpose(0, 2, 1, 3)

        def _layernorm(x, g, b):
            mu = jnp.mean(x, axis=-1, keepdims=True)
            var = jnp.mean(jnp.square(x - mu), axis=-1, keepdims=True)
            return (x - mu) * jax.lax.rsqrt(var + LN_EPS) * g + b
        q = x @ Wqk + bqk
        k = x @ Wqk + bqk
        v = jax.nn.silu(x @ Wv + bv)
        u = jax.nn.silu(x @ Wu + bu)
        q = jax.nn.elu(_heads(q))
        kh = jax.nn.elu(_heads(k))
        vh = _heads(v)
        kv = jnp.einsum('bhnd,bhne->bhde', kh, vh)
        out = jnp.einsum('bhnd,bhde->bhne', q, kv)
        out = out.transpose(0, 2, 1, 3).reshape(x.shape[0], x.shape[1], H_DIM)
        out = _layernorm(out, ln_g, ln_b)
        out = u * out
        return out @ Wo + bo

    def _L0_ffn_ref(x, gate_w, w1, w2, w3):
        import jax, jax.numpy as jnp
        import numpy as np
        NUM_ACT = 2
        B, S, D = x.shape
        xt = x.reshape(-1, D)
        scores = jnp.einsum('ti,ei->te', xt, gate_w)
        probs = jax.nn.softmax(scores, axis=-1)
        expert_weights, expert_indices = jax.lax.top_k(probs, NUM_ACT)
        expert_weights = expert_weights / expert_weights.sum(axis=-1, keepdims=True)
        x1 = jax.nn.silu(jnp.einsum('ti,eoi->teo', xt, w1))
        x3 = jnp.einsum('ti,eoi->teo', xt, w3)
        expert_outs_all = jnp.einsum('teo,eio->tei', x1 * x3, w2)
        sel = jnp.take_along_axis(expert_outs_all, expert_indices[:, :, None], axis=1)
        out = jnp.einsum('tai,ta->ti', sel, expert_weights)
        return out.reshape(B, S, D)
    x = L0_attn_x
    xn = _layernorm(x, axis=-1)
    x = x + _L0_attn_ref(xn, L0_attn_Wqk, L0_attn_bqk, L0_attn_Wv, L0_attn_bv, L0_attn_Wu, L0_attn_bu, L0_attn_Wo, L0_attn_bo, L0_attn_ln_g, L0_attn_ln_b) + _L0_ffn_ref(xn, L0_ffn_gate_w, L0_ffn_w1, L0_ffn_w2, L0_ffn_w3)
    return x

_drawn_inputs = setup_inputs


def setup_inputs(seed=0):
    import zlib

    import numpy as np

    out = dict(_drawn_inputs(seed))
    spreads = {'L0_attn_bqk': (0.0, 0.1),
     'L0_attn_bv': (0.0, 0.1),
     'L0_attn_bu': (0.0, 0.1),
     'L0_attn_bo': (0.0, 0.1),
     'L0_attn_ln_g': (1.0, 0.2),
     'L0_attn_ln_b': (0.0, 0.1)}
    factors = {'L0_ffn_gate_w': 4.509, 'L0_ffn_w1': 3.966, 'L0_ffn_w2': 3.923, 'L0_ffn_w3': 3.924}
    for name, (base, spread) in spreads.items():
        noise = np.random.default_rng([zlib.crc32(name.encode()), seed]).standard_normal(out[name].shape)
        drawn = base * np.exp(spread * noise) if base else spread * noise
        out[name] = jnp.asarray(drawn.astype(out[name].dtype))
    for name, factor in factors.items():
        out[name] = (out[name] * factor).astype(out[name].dtype)
    return out
```

```python
from contextlib import ExitStack

import concourse.bass as bass
from concourse import mybir

F32 = mybir.dt.float32
F16 = mybir.dt.float16
I32 = mybir.dt.int32
ALU = mybir.AluOpType
ACT = mybir.ActivationFunctionType
AX = mybir.AxisListType

P = 128
D = 256
KD = D // P
TOKENS = 2048
BATCHES = 2
TT = TOKENS // P
TB = TT // BATCHES
NP = TT // 2
HD = 16
E = 8
I = 512
IC = I // P
TOPK = 2
ST = TOPK * TOKENS // P + E - 1
PADS = ST - TOPK * TOKENS // P
WCOLS = 2 * KD * I + IC * D
W1, W3, W2 = 0, KD * I, 2 * KD * I
ROW = D + 2
AC = E + 4 * D
GATE, WU, WQ, WO = 0, E, E + D, E + 3 * D
SCALE = 64.0
KV_SCALE = 1.0 / 64.0
EPS = 1e-5
BIG = 1e30
CH = 4
NEWTON = 3
RSQRT_OPS = 2 + 3 * NEWTON


def build(nc, x, wattn, wexp, params, bias_rows, out):
    ctx = ExitStack()
    with ctx:
        def sb(name, shape, dt=F32):
            return ctx.enter_context(nc.sbuf_tensor(name, shape, dt))

        def psum(name):
            return ctx.enter_context(nc.psum_tensor(name, [P, 512], F32))

        def sem(name):
            return ctx.enter_context(nc.semaphore(name))

        def view(base, start, shape, dt=F32):
            n = 1
            for s in shape:
                n *= s
            words = n if dt != F16 else n // 2
            v = base[:, start:start + words]
            if dt != F32:
                v = v.bitcast(dt)
            if len(shape) == 2:
                v = v.rearrange("p (a b) -> p a b", b=shape[1])
            if len(shape) == 3:
                v = v.rearrange("p (a b c) -> p a b c", b=shape[1], c=shape[2])
            return v

        w16 = sb("w16", [P, E, 2, WCOLS], F16)
        stage = sb("stage", [P, 2 * WCOLS])
        attn32 = w16[:, E - 1, :, :].rearrange("p h c -> p (h c)").bitcast(F32)[:, 0:KD * AC]
        wa16 = sb("wa16", [P, 2, KD * AC], F16)
        area = sb("area", [P, TT * D])
        xrow = sb("xrow", [P, TT, ROW])
        xT = sb("xT", [P, 2 * KD, TOKENS], F16)
        kT = sb("kT", [P, 2 * KD, TOKENS], F16)
        xn32 = kT[:, :, :].rearrange("p c t -> p (c t)").bitcast(F32).rearrange("p (t d) -> p t d", d=D)
        padrow = sb("padrow", [P, ROW])
        qv_bias = sb("qv_bias", [P, 2 * D])
        o_bias = sb("o_bias", [P, D])
        par = sb("par", [P, 3, KD])
        ident = sb("ident", [P, P], F16)
        strict = sb("strict", [P, P], F16)
        ones = sb("ones", [P, P], F16)
        kv_mask = sb("kv_mask", [P, P])
        rev = sb("rev", [P, E])
        before = sb("before", [P, E, E])
        step128 = sb("step128", [P, TT])
        tile_no = sb("tile_no", [P, ST])
        pad_no = sb("pad_no", [P, PADS])
        stats = sb("stats", [P, TT, 6])
        mv = sb("mv", [P, TT, 2])
        rstd = sb("rstd", [P, TT])
        m16 = sb("m16", [P, TT, E], F16)
        slot = sb("slot", [P, TOPK, TT], I32)
        gate2 = sb("gate2", [P, TT])
        padslot = sb("padslot", [P, PADS], I32)
        tile_expert = sb("tile_expert", [P, ST], I32)
        kv16 = sb("kv16", [P, BATCHES, 2, KD * P], F16)
        kvm = sb("kvm", [P, KD, P])
        minus1 = sb("minus1", [P, 1])
        newton = sb("newton", [P, 2, CH])
        qv0 = [view(area, 512 * r, [2 * D]) for r in range(2)]
        eth = [view(area, 1024 + 512 * r, [2 * D]) for r in range(2)]
        kv32 = [view(area, 2048 + 512 * r, [2 * D]) for r in range(2)]
        kvrow = [view(area, 3072 + 512 * r, [4 * D], F16) for r in range(2)]
        uT = view(area, 0, [KD, 2 * P])
        n32 = view(area, 512, [2, D])
        n16 = view(area, 1024, [2, 2 * D], F16)
        yT = view(area, 1536, [KD, 2 * P])
        z32 = view(area, 2048, [KD * 2 * P])
        z16 = view(area, 2560, [2, KD * 2 * P], F16)
        fin = view(area, 3072, [2, D])
        stats2 = view(area, 3584, [2, 6])
        mv2 = view(area, 3600, [2, 2])
        rstd2 = view(area, 3608, [2])
        xg = [view(stage, 256 * r, [2 * KD, P], F16) for r in range(4)]
        meta = [view(stage, 1024 + 4 * r, [2]) for r in range(4)]
        s32 = [view(stage, 1040 + 512 * r, [I]) for r in range(2)]
        h32 = [view(stage, 2064 + 512 * r, [I]) for r in range(2)]
        h16 = [view(stage, 3088 + 512 * r, [2, I], F16) for r in range(2)]
        ysb = [view(stage, 4112 + 256 * r, [D]) for r in range(2)]

        bank = [psum(f"bank{i}") for i in range(8)]
        ps_gate, ps_route = bank[0], bank[1]
        ps_qv, ps_kv = bank[2:4], bank[4:6]
        ps_a, ps_b = bank[0:2], bank[2:4]
        ps_y = bank[4:6]
        ps_c0, ps_c1 = bank[6], bank[7]

        slots = nc.dram_tensor("slots", [ST * P, ROW], F32, kind="Internal").ap()

        x_first = sem("x_first")
        x_rest = sem("x_rest")
        attn_loaded = sem("attn_loaded")
        bias_loaded = sem("bias_loaded")
        stage0_loaded = sem("stage0_loaded")
        stage_loaded = sem("stage_loaded")
        pool_const = sem("pool_const")
        consts_ready = sem("consts_ready")
        bias_ready = sem("bias_ready")
        attn_hi = sem("attn_hi")
        attn_lo = sem("attn_lo")
        w_hi = sem("w_hi")
        w_lo = sem("w_lo")
        st_done = sem("st_done")
        mv_done = sem("mv_done")
        rstd_done = sem("rstd_done")
        xn_ready = sem("xn_ready")
        xh_ready = sem("xh_ready")
        xl_ready = sem("xl_ready")
        xT_done = [sem(f"xT_done{r}") for r in range(2)]
        scores_done = sem("scores_done")
        route_step = sem("route_step")
        gap_ready = sem("gap_ready")
        gexp_ready = sem("gexp_ready")
        mask_ready = sem("mask_ready")
        ranks_done = sem("ranks_done")
        gate_ready = sem("gate_ready")
        slot_ready = sem("slot_ready")
        scattered1 = sem("scattered1")
        gate2_placed = sem("gate2_placed")
        scattered2 = sem("scattered2")
        base_written = sem("base_written")
        qv_done = sem("qv_done")
        qv_taken = sem("qv_taken")
        exps_ready = sem("exps_ready")
        kv32_ready = sem("kv32_ready")
        kvh_ready = sem("kvh_ready")
        kvl_ready = sem("kvl_ready")
        kT_done = [sem(f"kT_done{r}") for r in range(2)]
        kv_mm = sem("kv_mm")
        kvm_ready = sem("kvm_ready")
        kv_hi = sem("kv_hi")
        kv_ready = sem("kv_ready")
        xg_loaded = [sem(f"xg_loaded{r}") for r in range(4)]
        a_done = sem("a_done")
        b_done = sem("b_done")
        s_ready = sem("s_ready")
        h_ready = sem("h_ready")
        hh_ready = sem("hh_ready")
        hl_ready = sem("hl_ready")
        y_done = sem("y_done")
        y_ready = sem("y_ready")
        y_added = sem("y_added")
        u_done = sem("u_done")
        uT_ready = sem("uT_ready")
        o_done = sem("o_done")
        c_stats = sem("c_stats")
        c_mv = sem("c_mv")
        c_rstd = sem("c_rstd")
        n_ready = sem("n_ready")
        nh_ready = sem("nh_ready")
        nl_ready = sem("nl_ready")
        nT_done = sem("nT_done")
        yT_ready = sem("yT_ready")
        z_ready = sem("z_ready")
        zh_ready = sem("zh_ready")
        zl_ready = sem("zl_ready")
        f_done = sem("f_done")
        fin_ready = sem("fin_ready")
        fin_added = sem("fin_added")
        held = sem("held")

        def wait(eng, semaphore, value):
            if not (isinstance(value, int) and value <= 0):
                eng.wait_ge(semaphore, value)

        def hold(eng, semaphore, value):
            eng.wait_ge(semaphore, value)
            eng.sem_inc(held, 1)

        x_tiles = x.rearrange("(t p) d -> p t d", p=P)
        out_pairs = out[0:TOKENS, :].rearrange("(i j p) d -> p i j d", j=2, p=P)
        slot_tiles = slots.rearrange("(s p) c -> p s c", p=P)
        slots16 = slots.bitcast(F16).rearrange("(s p) c -> s p c", p=P)
        xrow16 = xrow[:, :, 0:D].bitcast(F16)

        def loops(make):
            make(0, 0)
            return [(1, NP // BATCHES, 0), (NP // BATCHES, NP, 1)]

        block = ctx.enter_context(nc.Block())

        @block.sync
        def _(sp):
            sp.dma_start(view(area, 0, [CH, D]), x_tiles[:, 0:CH, :]).then_inc(x_first, 16)
            for c in range(1, TT // CH):
                sp.dma_start(view(area, c * CH * D, [CH, D]),
                             x_tiles[:, c * CH:(c + 1) * CH, :]).then_inc(x_rest, 16)
            sp.dma_start(par[:], params).then_inc(bias_loaded, 16)
            sp.dma_start(qv_bias[:], bias_rows[0:2 * D].partition_broadcast(P)).then_inc(bias_loaded, 16)
            sp.dma_start(o_bias[:], bias_rows[2 * D:3 * D].partition_broadcast(P)).then_inc(bias_loaded, 16)

            def transpose_x(i, first):
                for r in range(2):
                    t = 2 * i + r
                    if not first:
                        hold(sp, xT_done[r], 16 * i)
                    hold(sp, xl_ready, t + 1)
                    sp.dma_start_transpose(xT[:, :, bass.ds(t * P, P)],
                                           xrow16[:, bass.ds(t, 1), :].rearrange("p a c -> p (a c)")
                                           ).then_inc(xT_done[r], 16)
            transpose_x(0, True)
            with sp.Fori(1, NP) as i:
                transpose_x(i, False)

            sp.dma_start(out[0:TOKENS, :], x).then_inc(base_written, 16)
            sp.wait_ge(consts_ready, 1)
            sp.dma_start(out[TOKENS:TOKENS + P, :], padrow[:, 0:D]).then_inc(base_written, 16)

            def transpose_k(i, first):
                for r in range(2):
                    t = 2 * i + r
                    if not first:
                        hold(sp, kT_done[r], 16 * i)
                    hold(sp, kvl_ready, 2 * (t + 1))
                    sp.dma_start_transpose(kT[:, :, bass.ds(t * P, P)],
                                           kvrow[r][:, 0:2 * D]).then_inc(kT_done[r], 16)
            transpose_k(0, True)
            with sp.Fori(1, NP) as i:
                transpose_k(i, False)

            sp.wait_ge(scattered1, 16 * (TT + PADS))
            sp.wait_ge(scattered2, 16 * TT)
            sp.wait_ge(w_lo, E)

            def load_slots(t, r, first):
                if not first:
                    hold(sp, b_done, t - 3)
                    hold(sp, y_added, 16 * (t - 3))
                sp.dma_start_transpose(
                    xg[r], slots16[bass.ds(t, 1), :, 0:2 * D].rearrange("a p c -> (a p) c")
                ).then_inc(xg_loaded[r], 16)
                sp.dma_start(meta[r], slot_tiles[:, bass.ds(t, 1), D:ROW].rearrange("p a c -> p (a c)")
                             ).then_inc(xg_loaded[r], 16)
            for r in range(4):
                load_slots(r, r, True)
            with sp.Fori(1, NP) as i:
                for r in range(4):
                    load_slots(4 * i + r, r, False)
            for t in range(4 * NP, ST):
                load_slots(t, t % 4, False)
            sp.wait_ge(y_added, 16 * ST)
            sp.wait_ge(fin_added, 16 * NP)

        @block.gpsimd
        def _(pool):
            g = nc.gpsimd
            g.memset(ident[:], 0.0).then_inc(pool_const, 1)
            g.memset(strict[:], 1.0).then_inc(pool_const, 1)
            g.memset(kv_mask[:], 0.5 * KV_SCALE).then_inc(pool_const, 1)
            g.memset(before[:], 1.0).then_inc(pool_const, 1)
            g.memset(padrow[:], 0.0).then_inc(pool_const, 1)
            g.memset(ones[:], 1.0).then_inc(pool_const, 1)
            g.iota(rev[:], pattern=[[-1, E]], base=E, channel_multiplier=0,
                   allow_small_or_imprecise_dtypes=True).then_inc(pool_const, 1)
            g.iota(step128[:], pattern=[[P, TT]], base=0, channel_multiplier=0,
                   allow_small_or_imprecise_dtypes=True).then_inc(pool_const, 1)
            g.iota(tile_no[:], pattern=[[1, ST]], base=0, channel_multiplier=0,
                   allow_small_or_imprecise_dtypes=True).then_inc(pool_const, 1)
            g.iota(pad_no[:], pattern=[[P, PADS]], base=0, channel_multiplier=1,
                   allow_small_or_imprecise_dtypes=True).then_inc(pool_const, 1)
            g.iota(xrow[:, :, D:D + 1].bitcast(I32), pattern=[[P, TT], [0, 1]], base=0,
                   channel_multiplier=1).then_inc(pool_const, 1)
            pool.wait_ge(pool_const, 11)
            g.affine_select(out=ident[:], in_=ident[:], compare_op=ALU.not_equal, fill=1.0, base=0,
                            pattern=[[-1, P]], channel_multiplier=1).then_inc(pool_const, 1)
            g.affine_select(out=strict[:], in_=strict[:], compare_op=ALU.is_gt, fill=0.0, base=0,
                            pattern=[[1, P]], channel_multiplier=-1).then_inc(pool_const, 1)
            g.affine_select(out=before[:], in_=before[:], compare_op=ALU.is_gt, fill=0.0, base=0,
                            pattern=[[1, E], [-1, E]], channel_multiplier=0).then_inc(pool_const, 1)
            blocks = kv_mask[:, :].rearrange("p (g d) -> p g d", d=HD)
            g.affine_select(out=blocks, in_=blocks, compare_op=ALU.is_ge, fill=0.0, base=0,
                            pattern=[[-HD, P // HD], [0, HD]], channel_multiplier=1).then_inc(pool_const, 1)
            g.iota(padrow[:, D:D + 1].bitcast(I32), pattern=[[0, 1]], base=TOKENS,
                   channel_multiplier=1).then_inc(pool_const, 1)
            pool.wait_ge(pool_const, 16)
            g.affine_select(out=blocks, in_=blocks, compare_op=ALU.is_ge, fill=0.0, base=HD - 1,
                            pattern=[[HD, P // HD], [0, HD]], channel_multiplier=-1).then_inc(consts_ready, 1)

            with pool.Fori(0, TT) as t:
                pool.wait_ge(xh_ready, t + 1)
                g.tensor_tensor(xrow16[:, bass.ds(t, 1), D:2 * D], xn32[:, bass.ds(t, 1), :],
                                xrow16[:, bass.ds(t, 1), 0:D], ALU.subtract).then_inc(xl_ready, 1)

            def scatter(index, row):
                return g.indirect_dma_start(slots, bass.IndirectOffsetOnAxis(ap=index, axis=0), row, None)
            pool.wait_ge(slot_ready, 3)
            pool.wait_ge(xl_ready, TT)
            pool.wait_ge(gate_ready, 2)
            for t in range(TT):
                scatter(slot[:, 0, t:t + 1], xrow[:, t, :]).then_inc(scattered1, 16)
            for c in range(PADS):
                scatter(padslot[:, c:c + 1], padrow[:]).then_inc(scattered1, 16)
            pool.wait_ge(scattered1, 16 * (TT + PADS))
            g.tensor_copy(xrow[:, :, D + 1:D + 2], gate2[:].unsqueeze(2)).then_inc(gate2_placed, 1)
            pool.wait_ge(gate2_placed, 1)
            for t in range(TT):
                scatter(slot[:, 1, t:t + 1], xrow[:, t, :]).then_inc(scattered2, 16)

            def add_expert(t, r, r2):
                hold(pool, y_ready, t + 1)
                g.indirect_dma_start(out, bass.IndirectOffsetOnAxis(ap=meta[r][:, 0:1].bitcast(I32), axis=0),
                                     ysb[r2], None, compute_op=ALU.add).then_inc(y_added, 16)
                pool.wait_ge(y_added, 16 * (t + 1))

            def add_attention(p):
                hold(pool, fin_ready, p + 1)
                g.dma_start(out_pairs[:, bass.ds(p, 1), :, :].rearrange("p a j d -> p (a j) d"), fin,
                            accum_op=ALU.add).then_inc(fin_added, 16)
                pool.wait_ge(fin_added, 16 * (p + 1))

            def step(p, b):
                for r in range(4):
                    add_expert(4 * p + r, r, r % 2)
                add_attention(p)
            pool.wait_ge(base_written, 32)
            for lo, hi, b in loops(step):
                with pool.Fori(lo, hi) as p:
                    step(p, b)
            for t in range(4 * NP, ST):
                add_expert(t, t % 4, t % 2)

        @block.scalar
        def _(act):
            a = nc.scalar
            act.dma_start(attn32, wattn).then_inc(attn_loaded, 16)
            act.dma_start(stage[:, 0:WCOLS], wexp[0]).then_inc(stage0_loaded, 16)
            act.dma_start(stage[:, WCOLS:2 * WCOLS], wexp[1]).then_inc(stage_loaded, 16)

            def expert_hi(e):
                if isinstance(e, int) and e == 0:
                    act.wait_ge(stage0_loaded, 16)
                else:
                    act.wait_ge(stage_loaded, 16 * e)
                a.activation(w16[:, bass.ds(e, 1), 0, :].rearrange("p a c -> p (a c)"),
                             stage[:, bass.ds((e % 2) * WCOLS, WCOLS)], ACT.Copy,
                             scale=SCALE).then_inc(w_hi, 1)

            def load_expert(e):
                act.wait_ge(w_hi, e - 1)
                act.wait_ge(w_lo, e - 1)
                act.dma_start(stage[:, bass.ds((e % 2) * WCOLS, WCOLS)],
                              wexp[bass.ds(e, 1), :, :].rearrange("a p c -> (a p) c")
                              ).then_inc(stage_loaded, 16)

            def rows_hi(t):
                act.wait_ge(xn_ready, t + 1)
                a.activation(xrow16[:, bass.ds(t, 1), 0:D], xn32[:, bass.ds(t, 1), :],
                             ACT.Copy).then_inc(xh_ready, 1)
            with act.Fori(0, CH) as t:
                rows_hi(t)
            act.wait_ge(attn_loaded, 16)
            a.activation(wa16[:, 0, :], attn32, ACT.Copy, scale=SCALE).then_inc(attn_hi, 1)
            with act.Fori(CH, TT) as t:
                rows_hi(t)
            expert_hi(0)
            act.wait_ge(gap_ready, 1)
            a.activation(gate2[:], rstd[:], ACT.Exp).then_inc(gexp_ready, 1)

            def heads(i, first, expert):
                for r in range(2):
                    t = 2 * i + r
                    act.wait_ge(qv_taken, t + 1)
                    a.activation(eth[r][:, 0:D], qv0[r][:, 0:D], ACT.Exp, bias=minus1[:, 0:1]
                                 ).then_inc(exps_ready, 1)
                    a.activation(eth[r][:, D:2 * D], qv0[r][:, D:2 * D], ACT.Tanh, scale=0.5
                                 ).then_inc(exps_ready, 1)
                if expert:
                    expert_hi(i + 1)
                for r in range(2):
                    t = 2 * i + r
                    act.wait_ge(kv32_ready, 2 * (t + 1))
                    if not first:
                        act.wait_ge(kv_mm, t - 1)
                        act.wait_ge(kT_done[r], 16 * i)
                    a.activation(kvrow[r][:, 0:D], kv32[r][:, 0:D], ACT.Copy, bias=-1.0
                                 ).then_inc(kvh_ready, 1)
                    a.activation(kvrow[r][:, 2 * D:3 * D], kv32[r][:, D:2 * D], ACT.Copy
                                 ).then_inc(kvh_ready, 1)

            def kv_halves(b):
                act.wait_ge(kvm_ready, 2 * (b + 1))
                a.activation(kv16[:, b, 0, :], kvm[:, :, :].rearrange("p c d -> p (c d)"), ACT.Copy
                             ).then_inc(kv_hi, 1)

            heads(0, True, True)
            load_expert(2)
            with act.Fori(1, NP // 2) as i:
                heads(i, False, True)
                load_expert(i + 2)
            kv_halves(0)
            with act.Fori(NP // 2, NP - 2) as i:
                heads(i, False, True)
                load_expert(i + 2)
            heads(NP - 2, False, True)
            heads(NP - 1, False, False)
            kv_halves(1)

            def silu(t, r2):
                act.wait_ge(a_done, t + 1)
                wait(act, h_ready, t - 1)
                a.activation(s32[r2], ps_a[r2][:], ACT.Silu, scale=1.0 / SCALE).then_inc(s_ready, 1)

            def h_hi(t, r2):
                act.wait_ge(h_ready, t + 1)
                wait(act, y_done, t - 1)
                a.activation(h16[r2][:, 0, :], h32[r2], ACT.Copy).then_inc(hh_ready, 1)

            def y_out(t, r, r2):
                act.wait_ge(y_done, t + 1)
                wait(act, y_added, 16 * (t - 1))
                a.activation(ysb[r2], ps_y[r2][:, 0:D], ACT.Copy, scale=meta[r][:, 1:2]
                             ).then_inc(y_ready, 1)

            def u_gates(p):
                act.wait_ge(u_done, p + 1)
                wait(act, z_ready, p)
                for c in range(KD):
                    a.activation(uT[:, c, :], ps_c0[:, c * 2 * P:(c + 1) * 2 * P], ACT.Silu,
                                 bias=par[:, 0, c:c + 1], scale=1.0 / SCALE).then_inc(uT_ready, 1)

            def n_hi(p):
                act.wait_ge(n_ready, 2 * (p + 1))
                wait(act, nT_done, p)
                a.activation(n16[:, :, 0:D], n32, ACT.Copy).then_inc(nh_ready, 1)

            def y_norm(p):
                act.wait_ge(nT_done, p + 1)
                wait(act, z_ready, p)
                for c in range(KD):
                    a.activation(yT[:, c, :], ps_c0[:, c * 2 * P:(c + 1) * 2 * P], ACT.Identity,
                                 bias=par[:, 2, c:c + 1], scale=par[:, 1, c:c + 1]).then_inc(yT_ready, 1)

            def z_hi(p):
                act.wait_ge(z_ready, p + 1)
                wait(act, f_done, p)
                a.activation(z16[:, 0, :], z32, ACT.Copy).then_inc(zh_ready, 1)

            def step(p, b):
                t = 4 * p
                silu(t, 0)
                h_hi(t, 0)
                u_gates(p)
                silu(t + 1, 1)
                n_hi(p)
                h_hi(t + 1, 1)
                y_out(t, 0, 0)
                silu(t + 2, 0)
                h_hi(t + 2, 0)
                y_out(t + 1, 1, 1)
                y_norm(p)
                silu(t + 3, 1)
                z_hi(p)
                h_hi(t + 3, 1)
                y_out(t + 2, 2, 0)
                y_out(t + 3, 3, 1)
            act.wait_ge(w_lo, E)
            act.wait_ge(kT_done[0], 16 * NP)
            act.wait_ge(kT_done[1], 16 * NP)
            for lo, hi, b in loops(step):
                with act.Fori(lo, hi) as p:
                    step(p, b)
            for t in range(4 * NP, ST):
                silu(t, t % 2)
                h_hi(t, t % 2)
                if t > 4 * NP:
                    y_out(t - 1, (t - 1) % 4, (t - 1) % 2)
            y_out(ST - 1, (ST - 1) % 4, (ST - 1) % 2)

        @block.vector
        def _(dve):
            v = nc.vector
            v.memset(minus1[:], -1.0).then_inc(bias_ready, 1)

            def rsqrt(y, var, ve, sq, eps, done, call):
                n = [RSQRT_OPS * call]

                def link(instruction):
                    n[0] = n[0] + 1
                    instruction.then_inc(done, 1)
                    dve.wait_ge(done, n[0])
                link(v.tensor_scalar(ve, var, eps, None, ALU.add))
                link(v.tensor_scalar(y.bitcast(I32), ve.bitcast(I32), -0.5, float(0x5f3759df),
                                     ALU.mult, ALU.add))
                for _ in range(NEWTON):
                    link(v.tensor_tensor(sq, y, y, ALU.mult))
                    link(v.scalar_tensor_tensor(sq, sq, -0.5, ve, ALU.mult, ALU.mult))
                    link(v.scalar_tensor_tensor(y, sq, 1.5, y, ALU.add, ALU.mult))

            def norm(c):
                for k in range(CH):
                    v.bn_stats(stats[:, bass.ds(CH * c + k, 1), :].rearrange("p a s -> p (a s)"),
                               area[:, bass.ds((CH * c + k) * D, D)]).then_inc(st_done, 1)
                for k in range(CH):
                    dve.wait_ge(st_done, CH * c + k + 1)
                    v.bn_aggr(mv[:, bass.ds(CH * c + k, 1), :].rearrange("p a s -> p (a s)"),
                              stats[:, bass.ds(CH * c + k, 1), :].rearrange("p a s -> p (a s)")
                              ).then_inc(mv_done, 1)
                dve.wait_ge(mv_done, CH * (c + 1))
                rsqrt(rstd[:, bass.ds(CH * c, CH)], mv[:, bass.ds(CH * c, CH), 1:2].rearrange("p t a -> p (t a)"),
                      newton[:, 0, :], newton[:, 1, :], EPS, rstd_done, c)
                for k in range(CH):
                    v.tensor_scalar(xn32[:, bass.ds(CH * c + k, 1), :].rearrange("p a d -> p (a d)"),
                                    area[:, bass.ds((CH * c + k) * D, D)],
                                    mv[:, bass.ds(CH * c + k, 1), 0:1].rearrange("p a d -> p (a d)"),
                                    rstd[:, bass.ds(CH * c + k, 1)],
                                    ALU.subtract, ALU.mult).then_inc(xn_ready, 1)
            dve.wait_ge(x_first, 16)
            norm(0)
            dve.wait_ge(attn_hi, 1)
            v.scalar_tensor_tensor(wa16[:, 1, :], attn32, SCALE, wa16[:, 0, :], ALU.mult, ALU.subtract
                                   ).then_inc(attn_lo, 1)
            dve.wait_ge(x_rest, 16 * (TT // CH - 1))
            for c in range(1, TT // CH):
                norm(c)
            dve.wait_ge(bias_loaded, 48)
            v.tensor_scalar(qv_bias[:, 0:D], qv_bias[:, 0:D], 1.0, None, ALU.add).then_inc(bias_ready, 1)

            def expert_lo(e):
                dve.wait_ge(w_hi, e + 1)
                v.scalar_tensor_tensor(w16[:, bass.ds(e, 1), 1, :].rearrange("p a c -> p (a c)"),
                                       stage[:, bass.ds((e % 2) * WCOLS, WCOLS)], SCALE,
                                       w16[:, bass.ds(e, 1), 0, :].rearrange("p a c -> p (a c)"),
                                       ALU.mult, ALU.subtract).then_inc(w_lo, 1)
            expert_lo(0)

            at = [0]

            def tmp(shape):
                n = 1
                for s in shape:
                    n *= s
                at[0] += n
                return view(area, at[0] - n, shape)
            count = [0]

            def chain(instruction):
                count[0] += 1
                instruction.then_inc(route_step, 1)
                dve.wait_ge(route_step, count[0])

            sc, sc2, pick, hit1, hit2, dest, part = [tmp([TT, E]) for _ in range(7)]
            first, second, i1, i2, gap, ge1 = [tmp([TT]) for _ in range(6)]
            slotf = tmp([TOPK, TT])
            total, tiles, base, end, rows, freed = [tmp([E]) for _ in range(6)]
            over = tmp([E, TT])
            sums = tmp([E, E])
            expf = tmp([ST, E - 1])
            expn = tmp([ST])
            padf = tmp([PADS, E])
            padn = tmp([PADS])

            def per_tile(u):
                return u.unsqueeze(2).broadcast_to([P, TT, E])

            def per_expert(u):
                return u.unsqueeze(1).broadcast_to([P, TT, E])
            dve.wait_ge(consts_ready, 1)
            dve.wait_ge(scores_done, NP)
            chain(v.tensor_scalar(sc, ps_gate[:, 0:TT * E].rearrange("p (t e) -> p t e", e=E),
                                  1.0 / SCALE, None, ALU.mult))
            chain(v.tensor_reduce(first, sc, AX.X, ALU.max))
            chain(v.tensor_tensor(hit1, sc, per_tile(first), ALU.is_equal))
            chain(v.tensor_tensor(pick, hit1, per_expert(rev[:]), ALU.mult))
            chain(v.tensor_reduce(i1, pick, AX.X, ALU.max))
            chain(v.tensor_tensor(hit1, per_expert(rev[:]), per_tile(i1), ALU.is_equal))
            chain(v.scalar_tensor_tensor(sc2, hit1, -BIG, sc, ALU.mult, ALU.add))
            chain(v.tensor_reduce(second, sc2, AX.X, ALU.max))
            v.tensor_tensor(rstd[:], second, first, ALU.subtract).then_inc(gap_ready, 1)
            chain(v.tensor_tensor(hit2, sc2, per_tile(second), ALU.is_equal))
            chain(v.tensor_tensor(pick, hit2, per_expert(rev[:]), ALU.mult))
            chain(v.tensor_reduce(i2, pick, AX.X, ALU.max))
            chain(v.tensor_tensor(hit2, per_expert(rev[:]), per_tile(i2), ALU.is_equal))
            v.tensor_tensor(m16[:], hit1, hit2, ALU.add).then_inc(mask_ready, 1)
            dve.wait_ge(gexp_ready, 1)
            chain(v.tensor_scalar(ge1, gate2[:], SCALE, SCALE, ALU.mult, ALU.add))
            chain(v.reciprocal(gap, ge1))
            v.tensor_copy(xrow[:, :, D + 1:D + 2], gap.unsqueeze(2)).then_inc(gate_ready, 1)
            v.tensor_tensor(gate2[:], gate2[:], gap, ALU.mult).then_inc(gate_ready, 1)
            dve.wait_ge(ranks_done, 1)
            chain(v.tensor_copy(total, ps_route[:, TT * E:TT * E + E]))
            chain(v.tensor_tensor(over, total.unsqueeze(2).broadcast_to([P, E, TT]),
                                  step128[:].unsqueeze(1).broadcast_to([P, E, TT]), ALU.is_gt))
            chain(v.tensor_reduce(tiles, over, AX.X, ALU.add))
            chain(v.tensor_tensor(sums, before[:], tiles.unsqueeze(1).broadcast_to([P, E, E]), ALU.mult))
            chain(v.tensor_reduce(base, sums, AX.X, ALU.add))
            chain(v.scalar_tensor_tensor(dest, per_expert(base), float(P),
                                         ps_route[:, 0:TT * E].rearrange("p (t e) -> p t e", e=E),
                                         ALU.mult, ALU.add))
            for k, hit in enumerate((hit1, hit2)):
                chain(v.tensor_tensor(part, hit, dest, ALU.mult))
                chain(v.tensor_reduce(slotf[:, k, :], part, AX.X, ALU.add))
            v.tensor_copy(slot[:], slotf).then_inc(slot_ready, 1)
            chain(v.tensor_tensor(sums, before[:], total.unsqueeze(1).broadcast_to([P, E, E]), ALU.mult))
            chain(v.tensor_reduce(rows, sums, AX.X, ALU.add))
            chain(v.scalar_tensor_tensor(freed, base, float(P), rows, ALU.mult, ALU.subtract))
            chain(v.tensor_tensor(padf, pad_no[:].unsqueeze(2).broadcast_to([P, PADS, E]),
                                  freed.unsqueeze(1).broadcast_to([P, PADS, E]), ALU.is_ge))
            chain(v.tensor_tensor(padf, padf, total.unsqueeze(1).broadcast_to([P, PADS, E]), ALU.mult))
            chain(v.tensor_reduce(padn, padf, AX.X, ALU.add))
            v.tensor_tensor(padslot[:], padn, pad_no[:], ALU.add).then_inc(slot_ready, 1)
            chain(v.tensor_tensor(end, base, tiles, ALU.add))
            chain(v.tensor_tensor(expf, end[:, 0:E - 1].unsqueeze(1).broadcast_to([P, ST, E - 1]),
                                  tile_no[:].unsqueeze(2).broadcast_to([P, ST, E - 1]), ALU.is_le))
            chain(v.tensor_reduce(expn, expf, AX.X, ALU.add))
            v.tensor_copy(tile_expert[:], expn).then_inc(slot_ready, 1)

            dve.wait_ge(bias_ready, 2)
            dve.wait_ge(slot_ready, 3)

            def heads(i, first, expert):
                for r in range(2):
                    t = 2 * i + r
                    dve.wait_ge(qv_done, t + 1)
                    v.scalar_tensor_tensor(qv0[r], ps_qv[r][:], 1.0 / SCALE, qv_bias[:],
                                           ALU.mult, ALU.add).then_inc(qv_taken, 1)
                for r in range(2):
                    t = 2 * i + r
                    dve.wait_ge(exps_ready, 2 * (t + 1))
                    dve.wait_ge(qv_taken, t + 1)
                    v.scalar_tensor_tensor(kv32[r][:, 0:D], eth[r][:, 0:D], 1.0, qv0[r][:, 0:D],
                                           ALU.min, ALU.max).then_inc(kv32_ready, 1)
                    v.scalar_tensor_tensor(kv32[r][:, D:2 * D], eth[r][:, D:2 * D], 1.0,
                                           qv0[r][:, D:2 * D], ALU.add, ALU.mult).then_inc(kv32_ready, 1)
                if expert:
                    expert_lo(i + 1)
                for r in range(2):
                    t = 2 * i + r
                    dve.wait_ge(kvh_ready, 2 * (t + 1))
                    v.scalar_tensor_tensor(kvrow[r][:, D:2 * D], kv32[r][:, 0:D], -1.0,
                                           kvrow[r][:, 0:D], ALU.add, ALU.subtract).then_inc(kvl_ready, 1)
                    v.tensor_tensor(kvrow[r][:, 3 * D:4 * D], kv32[r][:, D:2 * D],
                                    kvrow[r][:, 2 * D:3 * D], ALU.subtract).then_inc(kvl_ready, 1)

            def kv_halves(b):
                dve.wait_ge(kv_mm, TB * (b + 1))
                for c in range(KD):
                    v.tensor_tensor(kvm[:, c, :], ps_kv[c][:, 0:P], kv_mask[:], ALU.mult
                                    ).then_inc(kvm_ready, 1)
                dve.wait_ge(kv_hi, b + 1)
                v.tensor_tensor(kv16[:, b, 1, :], kvm[:, :, :].rearrange("p c d -> p (c d)"),
                                kv16[:, b, 0, :], ALU.subtract).then_inc(kv_ready, 1)

            heads(0, True, True)
            with dve.Fori(1, NP // 2) as i:
                heads(i, False, True)
            kv_halves(0)
            with dve.Fori(NP // 2, NP - 1) as i:
                heads(i, False, True)
            heads(NP - 1, False, False)
            kv_halves(1)

            def h_mul(t, r2):
                dve.wait_ge(b_done, t + 1)
                dve.wait_ge(s_ready, t + 1)
                wait(dve, hh_ready, t - 1)
                v.scalar_tensor_tensor(h32[r2], ps_b[r2][:], 1.0 / SCALE, s32[r2],
                                       ALU.mult, ALU.mult).then_inc(h_ready, 1)

            def h_lo(t, r2):
                dve.wait_ge(hh_ready, t + 1)
                v.tensor_tensor(h16[r2][:, 1, :], h32[r2], h16[r2][:, 0, :], ALU.subtract
                                ).then_inc(hl_ready, 1)

            def center(p):
                dve.wait_ge(o_done, p + 1)
                for j in range(2):
                    v.bn_stats(stats2[:, j, :], ps_c1[:, j * D:(j + 1) * D]).then_inc(c_stats, 1)
                for j in range(2):
                    hold(dve, c_stats, 2 * p + j + 1)
                    v.bn_aggr(mv2[:, j, :], stats2[:, j, :]).then_inc(c_mv, 1)
                dve.wait_ge(c_mv, 2 * p + 2)
                rsqrt(rstd2, mv2[:, :, 1:2].rearrange("p t a -> p (t a)"), newton[:, 0, 0:2],
                      newton[:, 1, 0:2], EPS * KV_SCALE * KV_SCALE, c_rstd, p)
                for j in range(2):
                    v.tensor_scalar(n32[:, j, :], ps_c1[:, j * D:(j + 1) * D], mv2[:, j, 0:1],
                                    rstd2[:, j:j + 1], ALU.subtract, ALU.mult).then_inc(n_ready, 1)

            def n_lo(p):
                dve.wait_ge(nh_ready, p + 1)
                v.tensor_tensor(n16[:, :, D:2 * D], n32, n16[:, :, 0:D], ALU.subtract
                                ).then_inc(nl_ready, 1)

            def z_mul(p):
                dve.wait_ge(yT_ready, 2 * (p + 1))
                dve.wait_ge(uT_ready, 2 * (p + 1))
                v.tensor_tensor(z32, yT[:, :, :].rearrange("p c t -> p (c t)"),
                                uT[:, :, :].rearrange("p c t -> p (c t)"), ALU.mult).then_inc(z_ready, 1)

            def z_lo(p):
                dve.wait_ge(zh_ready, p + 1)
                v.tensor_tensor(z16[:, 1, :], z32, z16[:, 0, :], ALU.subtract).then_inc(zl_ready, 1)

            def finish(p):
                dve.wait_ge(f_done, p + 1)
                wait(dve, fin_added, 16 * p)
                v.scalar_tensor_tensor(fin, ps_c1[:, :].rearrange("p (j d) -> p j d", d=D), 1.0 / SCALE,
                                       o_bias[:].unsqueeze(1).broadcast_to([P, 2, D]),
                                       ALU.mult, ALU.add).then_inc(fin_ready, 1)

            def step(p, b):
                t = 4 * p
                h_mul(t, 0)
                h_lo(t, 0)
                center(p)
                h_mul(t + 1, 1)
                h_lo(t + 1, 1)
                n_lo(p)
                h_mul(t + 2, 0)
                h_lo(t + 2, 0)
                z_mul(p)
                h_mul(t + 3, 1)
                z_lo(p)
                h_lo(t + 3, 1)
                finish(p)
            dve.wait_ge(w_lo, E)
            dve.wait_ge(kT_done[0], 16 * NP)
            dve.wait_ge(kT_done[1], 16 * NP)
            for lo, hi, b in loops(step):
                with dve.Fori(lo, hi) as p:
                    step(p, b)
            for t in range(4 * NP, ST):
                h_mul(t, t % 2)
                h_lo(t, t % 2)

        @block.tensor
        def _(pe):
            mm = nc.tensor.matmul
            PASSES = ((0, 0), (0, 1), (1, 0))

            pe.wait_ge(attn_lo, 1)
            with pe.Fori(0, NP) as i:
                for r in range(2):
                    pe.wait_ge(xT_done[r], 16 * (i + 1))
                    for k in range(KD):
                        for n, (w, d) in enumerate(PASSES):
                            last = mm(ps_gate[:, bass.ds((2 * i + r) * E, E)],
                                      xT[:, KD * d + k, bass.ds((2 * i + r) * P, P)],
                                      wa16[:, w, k * AC + GATE:k * AC + GATE + E],
                                      start=(k == 0 and n == 0), stop=(k == KD - 1 and n == 2))
                last.then_inc(scores_done, 1)

            pe.wait_ge(mask_ready, 1)
            mm(ps_route[:, 0:TT * E], strict[:], m16[:, :, :].rearrange("p t e -> p (t e)"),
               start=True, stop=False)
            for s in range(1, TT):
                mm(ps_route[:, s * E:TT * E], ones[:], m16[:, 0:TT - s, :].rearrange("p t e -> p (t e)"),
                   start=False, stop=(s == TT - 1))
            for s in range(TT):
                last = mm(ps_route[:, TT * E:TT * E + E], ones[:], m16[:, s, :],
                          start=(s == 0), stop=(s == TT - 1))
            last.then_inc(ranks_done, 1)

            def qv(t, r):
                wait(pe, qv_taken, t - 1)
                for k in range(KD):
                    for n, (w, d) in enumerate(PASSES):
                        last = mm(ps_qv[r][:], xT[:, KD * d + k, bass.ds(t * P, P)],
                                  wa16[:, w, k * AC + WQ:k * AC + WQ + 2 * D],
                                  start=(k == 0 and n == 0), stop=(k == KD - 1 and n == 2))
                last.then_inc(qv_done, 1)

            def kv(t, r, start, stop):
                pe.wait_ge(kvl_ready, 2 * (t + 1))
                for c in range(KD):
                    for n, (w, d) in enumerate(PASSES):
                        last = mm(ps_kv[c][:, 0:P], kvrow[r][:, w * D + c * P:w * D + (c + 1) * P],
                                  kvrow[r][:, (2 + d) * D + c * P:(2 + d) * D + (c + 1) * P],
                                  start=(start and n == 0), stop=(stop and n == 2), skip_group_check=True)
                last.then_inc(kv_mm, 1)

            def batch(b):
                i0 = b * NP // 2
                qv(2 * i0, 0)
                qv(2 * i0 + 1, 1)
                if b > 0:
                    pe.wait_ge(kvm_ready, 2 * b)
                kv(2 * i0, 0, True, False)
                with pe.Fori(i0 + 1, i0 + NP // 2) as i:
                    qv(2 * i, 0)
                    kv(2 * i - 1, 1, False, False)
                    qv(2 * i + 1, 1)
                    kv(2 * i, 0, False, False)
                kv(2 * (i0 + NP // 2) - 1, 1, False, True)
            batch(0)
            batch(1)

            def hidden(t, r, r2, visit):
                pe.wait_ge(xg_loaded[r], 32 * (visit + 1))
                e = pe.value_load(tile_expert[0:1, bass.ds(t, 1)], min_val=0, max_val=E - 1)
                for bank_, col, done, taken in ((ps_a[r2], W1, a_done, s_ready), (ps_b[r2], W3, b_done, h_ready)):
                    wait(pe, taken, t - 1)
                    for c in range(IC):
                        for k in range(KD):
                            at = col + k * I + c * P
                            for n, (w, d) in enumerate(PASSES):
                                last = mm(bank_[:, c * P:(c + 1) * P],
                                          w16[:, bass.ds(e, 1), w, at:at + P].rearrange("p a c -> p (a c)"),
                                          xg[r][:, KD * d + k, :],
                                          start=(k == 0 and n == 0), stop=(k == KD - 1 and n == 2))
                    last.then_inc(done, 1)
                return e

            def down(t, e, r2):
                pe.wait_ge(hl_ready, t + 1)
                wait(pe, y_ready, t - 1)
                for c in range(IC):
                    at = W2 + c * D
                    for n, (w, d) in enumerate(PASSES):
                        last = mm(ps_y[r2][:, 0:D], h16[r2][:, d, c * P:(c + 1) * P],
                                  w16[:, bass.ds(e, 1), w, at:at + D].rearrange("p a c -> p (a c)"),
                                  start=(c == 0 and n == 0), stop=(c == IC - 1 and n == 2))
                last.then_inc(y_done, 1)

            def u_proj(p):
                wait(pe, yT_ready, 2 * p)
                for c in range(KD):
                    for k in range(KD):
                        at = k * AC + WU + c * P
                        for n, (w, d) in enumerate(PASSES):
                            last = mm(ps_c0[:, c * 2 * P:(c + 1) * 2 * P], wa16[:, w, at:at + P],
                                      xT[:, KD * d + k, bass.ds(p * 2 * P, 2 * P)],
                                      start=(k == 0 and n == 0), stop=(k == KD - 1 and n == 2))
                last.then_inc(u_done, 1)

            def q_kv(p, b):
                wait(pe, fin_ready, p)
                for j in range(2):
                    for c in range(KD):
                        for n, (w, d) in enumerate(PASSES):
                            last = mm(ps_c1[:, j * D + c * P:j * D + (c + 1) * P],
                                      kT[:, KD * d + c, bass.ds((2 * p + j) * P, P)],
                                      kv16[:, b, w, c * P:(c + 1) * P],
                                      start=(n == 0), stop=(n == 2))
                last.then_inc(o_done, 1)

            def turn(p):
                pe.wait_ge(nl_ready, p + 1)
                pe.wait_ge(uT_ready, 2 * (p + 1))
                for c in range(KD):
                    for j in range(2):
                        for w in range(2):
                            last = mm(ps_c0[:, c * 2 * P + j * P:c * 2 * P + (j + 1) * P],
                                      n16[:, j, w * D + c * P:w * D + (c + 1) * P], ident[:],
                                      start=(w == 0), stop=(w == 1))
                last.then_inc(nT_done, 1)

            def project(p):
                pe.wait_ge(zl_ready, p + 1)
                for j in range(2):
                    for c in range(KD):
                        at = c * AC + WO
                        for n, (w, d) in enumerate(PASSES):
                            last = mm(ps_c1[:, j * D:(j + 1) * D],
                                      z16[:, d, c * 2 * P + j * P:c * 2 * P + (j + 1) * P],
                                      wa16[:, w, at:at + D],
                                      start=(c == 0 and n == 0), stop=(c == KD - 1 and n == 2))
                last.then_inc(f_done, 1)

            def step(p, b):
                t = 4 * p
                e0 = hidden(t, 0, 0, p)
                u_proj(p)
                q_kv(p, b)
                e1 = hidden(t + 1, 1, 1, p)
                down(t, e0, 0)
                e2 = hidden(t + 2, 2, 0, p)
                down(t + 1, e1, 1)
                turn(p)
                e3 = hidden(t + 3, 3, 1, p)
                down(t + 2, e2, 0)
                project(p)
                down(t + 3, e3, 1)
            pe.wait_ge(slot_ready, 3)
            pe.wait_ge(w_lo, E)
            pe.wait_ge(kv_ready, BATCHES)
            pe.wait_ge(kT_done[0], 16 * NP)
            pe.wait_ge(kT_done[1], 16 * NP)
            for lo, hi, b in loops(step):
                with pe.Fori(lo, hi) as p:
                    step(p, b)
            before_e = None
            for t in range(4 * NP, ST):
                e = hidden(t, t % 4, t % 2, t // 4)
                if before_e is not None:
                    down(t - 1, before_e, (t - 1) % 2)
                before_e = e
            down(ST - 1, before_e, (ST - 1) % 2)


def kernel(**inputs):
    import numpy as np
    import concourse.bacc as bacc
    from concourse.bass_utils import run_bass_kernel_spmd

    def get(name):
        return np.ascontiguousarray(inputs["L0_" + name])

    x = get("attn_x")
    shape = x.shape
    rows = [get("ffn_gate_w").T, get("attn_Wu"), get("attn_Wqk"), get("attn_Wv"), get("attn_Wo")]
    wattn = np.concatenate(rows, axis=1).reshape(KD, P, AC).transpose(1, 0, 2).reshape(P, KD * AC)

    def chunks(w):
        e, k, m = w.shape
        return w.reshape(e, k // P, P, m).transpose(0, 2, 1, 3).reshape(e, P, k // P * m)
    wexp = np.concatenate([chunks(get("ffn_w1").transpose(0, 2, 1)), chunks(get("ffn_w3").transpose(0, 2, 1)),
                           chunks(get("ffn_w2").transpose(0, 2, 1))], axis=2)
    params = np.stack([get(n).reshape(KD, P).T for n in ("attn_bu", "attn_ln_g", "attn_ln_b")], axis=1)
    bias_rows = np.concatenate([get("attn_bqk"), get("attn_bv"), get("attn_bo")])
    arrays = {"x": x.reshape(TOKENS, D), "wattn": wattn, "wexp": wexp, "params": params,
              "bias_rows": bias_rows}
    arrays = {n: np.ascontiguousarray(a) for n, a in arrays.items()}

    nc = bacc.Bacc("TRN2", target_bir_lowering=False, num_devices=1)
    args = [nc.dram_tensor(n, a.shape, mybir.dt.from_np(a.dtype), kind="ExternalInput").ap()
            for n, a in arrays.items()]
    out = nc.dram_tensor("out", (TOKENS + P, D), F32, kind="ExternalOutput").ap()
    build(nc, *args, out)
    r = run_bass_kernel_spmd(nc, [arrays], core_ids=[0])
    return r.results[0]["out"][0:TOKENS].reshape(shape)
```

```python
import math
from contextlib import ExitStack

import concourse.bass as bass
from concourse import mybir

F32 = mybir.dt.float32
F16 = mybir.dt.float16
I32 = mybir.dt.int32
ALU = mybir.AluOpType
ACT = mybir.ActivationFunctionType
AX = mybir.AxisListType

P = 128
D = 256
KD = D // P
TOKENS = 2048
BATCHES = 2
TT = TOKENS // P
TB = TT // BATCHES
NP = TT // 2
HD = 16
E = 8
I = 512
IC = I // P
TOPK = 2
ST = TOPK * TOKENS // P + E - 1
PADS = ST - TOPK * TOKENS // P
WCOLS = 2 * KD * I + IC * D
W1, W3, W2 = 0, KD * I, 2 * KD * I
ROW = D + 2
AC = E + 4 * D
GATE, WU, WQ, WO = 0, E, E + D, E + 3 * D
SCALE = 64.0
K_SCALE = SCALE
V_SCALE = 2.0 * SCALE
KV_SCALE = 1.0 / K_SCALE
EPS = 1e-5
BIG = 1e30
CH = 4
NEWTON = 3
RSQRT_OPS = 2 + 3 * NEWTON


def build(nc, x, wattn, wexp, params, bias_rows, out):
    ctx = ExitStack()
    with ctx:
        def sb(name, shape, dt=F32):
            return ctx.enter_context(nc.sbuf_tensor(name, shape, dt))

        def psum(name):
            return ctx.enter_context(nc.psum_tensor(name, [P, 512], F32))

        def sem(name):
            return ctx.enter_context(nc.semaphore(name))

        def view(base, start, shape, dt=F32):
            n = 1
            for s in shape:
                n *= s
            words = n if dt != F16 else n // 2
            v = base[:, start:start + words]
            if dt != F32:
                v = v.bitcast(dt)
            if len(shape) == 2:
                v = v.rearrange("p (a b) -> p a b", b=shape[1])
            if len(shape) == 3:
                v = v.rearrange("p (a b c) -> p a b c", b=shape[1], c=shape[2])
            return v

        w16 = sb("w16", [P, E, 2, WCOLS], F16)
        stage = sb("stage", [P, 2 * WCOLS])
        attn32 = w16[:, E - 1, :, :].rearrange("p h c -> p (h c)").bitcast(F32)[:, 0:KD * AC]
        wa16 = sb("wa16", [P, 2, KD * AC], F16)
        area = sb("area", [P, TT * D])
        xrow = sb("xrow", [P, TT, ROW])
        xT = sb("xT", [P, 2 * KD, TOKENS], F16)
        kT = sb("kT", [P, 2 * KD, TOKENS], F16)
        xn32 = kT[:, :, :].rearrange("p c t -> p (c t)").bitcast(F32).rearrange("p (t d) -> p t d", d=D)
        padrow = sb("padrow", [P, ROW])
        qv_bias = sb("qv_bias", [1, 2 * D])
        qv_bias16 = sb("qv_bias16", [1, 2, 2 * D], F16)
        o_bias = sb("o_bias", [P, D])
        par = sb("par", [P, 3, KD])
        ident = sb("ident", [P, P], F16)
        strict = sb("strict", [P, P], F16)
        ones = sb("ones", [P, P], F16)
        kv_mask = sb("kv_mask", [P, P])
        rev = sb("rev", [P, E])
        before = sb("before", [P, E, E])
        step128 = sb("step128", [P, TT])
        tile_no = sb("tile_no", [P, ST])
        pad_no = sb("pad_no", [P, PADS])
        stats = sb("stats", [P, TT, 6])
        mv = sb("mv", [P, TT, 2])
        rstd = sb("rstd", [P, TT])
        m16 = sb("m16", [P, TT, E], F16)
        slot = sb("slot", [P, TOPK, TT], I32)
        gap_in = sb("gap_in", [P, TT])
        gate2 = sb("gate2", [P, TT])
        warm = sb("warm", [P, 1])
        padslot = sb("padslot", [P, PADS], I32)
        tile_expert = sb("tile_expert", [P, ST], I32)
        kv16 = sb("kv16", [P, BATCHES, 2, KD * P], F16)
        kvm = sb("kvm", [P, KD, P])
        log_scale = sb("log_scale", [P, 1])
        newton = sb("newton", [P, 2, TT])
        shift = sb("shift", [P, TT])
        eth = [view(area, 1024 + 512 * r, [2 * D]) for r in range(2)]
        kv32 = [view(area, 2048 + 512 * r, [2 * D]) for r in range(2)]
        kvrow = [view(area, 3072 + 512 * r, [4 * D], F16) for r in range(2)]
        uT = view(area, 0, [KD, 2 * P])
        n32 = view(area, 512, [2, D])
        n16 = view(area, 1024, [2, 2 * D], F16)
        yT = view(area, 1536, [KD, 2 * P])
        z32 = view(area, 2048, [KD * 2 * P])
        z16 = view(area, 2560, [2, KD * 2 * P], F16)
        fin = view(area, 3072, [2, D])
        stats2 = view(area, 3584, [2, 6])
        mv2 = view(area, 3600, [2, 2])
        rstd2 = view(area, 3608, [2])
        xg = [view(stage, 256 * r, [2 * KD, P], F16) for r in range(4)]
        meta = [view(stage, 1024 + 4 * r, [2]) for r in range(4)]
        s32 = [view(stage, 1040 + 512 * r, [I]) for r in range(2)]
        h32 = [view(stage, 2064 + 512 * r, [I]) for r in range(2)]
        h16 = [view(stage, 3088 + 512 * r, [2, I], F16) for r in range(2)]
        ysb = [view(stage, 4112 + 256 * r, [D]) for r in range(2)]
        hT = [view(stage, 4624 + 512 * r, [2 * IC, P], F16) for r in range(2)]

        bank = [psum(f"bank{i}") for i in range(8)]
        ps_gate, ps_route = bank[0], bank[1]
        ps_qv, ps_kv = bank[2:4], bank[4:6]
        ps_a, ps_b = bank[0:2], bank[2:4]
        ps_y = bank[4:6]
        ps_c0, ps_c1 = bank[6], bank[7]

        slots = nc.dram_tensor("slots", [ST * P, ROW], F32, kind="Internal").ap()

        x_first = sem("x_first")
        x_rest = sem("x_rest")
        attn_loaded = sem("attn_loaded")
        bias_loaded = sem("bias_loaded")
        stage0_loaded = sem("stage0_loaded")
        stage_loaded = sem("stage_loaded")
        pool_const = sem("pool_const")
        consts_ready = sem("consts_ready")
        bias_ready = sem("bias_ready")
        bias_hi = sem("bias_hi")
        bias_lo = sem("bias_lo")
        warm_done = sem("warm_done")
        attn_hi = sem("attn_hi")
        attn_lo = sem("attn_lo")
        w_hi = sem("w_hi")
        w_scaled = sem("w_scaled")
        w_lo_pool = sem("w_lo_pool")
        w_lo = sem("w_lo")
        shift_ready = sem("shift_ready")
        st_done = sem("st_done")
        mv_done = sem("mv_done")
        rstd_done = sem("rstd_done")
        xn_ready = sem("xn_ready")
        xh_ready = sem("xh_ready")
        xl_ready = sem("xl_ready")
        xT_done = [sem(f"xT_done{r}") for r in range(CH)]
        scores_done = sem("scores_done")
        route_step = sem("route_step")
        gap_ready = sem("gap_ready")
        gexp_ready = sem("gexp_ready")
        mask_ready = sem("mask_ready")
        ranks_done = sem("ranks_done")
        gate_ready = sem("gate_ready")
        slot_ready = sem("slot_ready")
        scattered1 = sem("scattered1")
        gate2_placed = sem("gate2_placed")
        scattered2 = sem("scattered2")
        base_written = sem("base_written")
        qv_done = sem("qv_done")
        exps_ready = sem("exps_ready")
        kv32_ready = sem("kv32_ready")
        kvh_ready = sem("kvh_ready")
        kvl_ready = sem("kvl_ready")
        kT_done = [sem(f"kT_done{r}") for r in range(2)]
        kv_mm = sem("kv_mm")
        kvm_ready = sem("kvm_ready")
        kv_hi = sem("kv_hi")
        kv_ready = sem("kv_ready")
        xg_loaded = [sem(f"xg_loaded{r}") for r in range(4)]
        meta_loaded = [sem(f"meta_loaded{r}") for r in range(4)]
        hT_done = [sem(f"hT_done{r}") for r in range(2)]
        a_done = sem("a_done")
        b_done = sem("b_done")
        s_ready = sem("s_ready")
        h_ready = sem("h_ready")
        hh_ready = sem("hh_ready")
        hl_ready = sem("hl_ready")
        y_done = sem("y_done")
        y_ready = sem("y_ready")
        y_added = sem("y_added")
        u_done = sem("u_done")
        uT_ready = sem("uT_ready")
        o_done = sem("o_done")
        c_stats = sem("c_stats")
        c_mv = sem("c_mv")
        c_rstd = sem("c_rstd")
        n_ready = sem("n_ready")
        nh_ready = sem("nh_ready")
        nl_ready = sem("nl_ready")
        nT_done = sem("nT_done")
        yT_ready = sem("yT_ready")
        z_ready = sem("z_ready")
        zh_ready = sem("zh_ready")
        zl_ready = sem("zl_ready")
        f_done = sem("f_done")
        fin_ready = sem("fin_ready")
        fin_added = sem("fin_added")
        held = sem("held")

        def wait(eng, semaphore, value):
            if not (isinstance(value, int) and value <= 0):
                eng.wait_ge(semaphore, value)

        def hold(eng, semaphore, value):
            eng.wait_ge(semaphore, value)
            eng.sem_inc(held, 1)

        x_tiles = x.rearrange("(t p) d -> p t d", p=P)
        out_pairs = out[0:TOKENS, :].rearrange("(i j p) d -> p i j d", j=2, p=P)
        slot_tiles = slots.rearrange("(s p) c -> p s c", p=P)
        slots16 = slots.bitcast(F16).rearrange("(s p) c -> s p c", p=P)
        xrow16 = xrow[:, :, 0:D].bitcast(F16)

        def loops(make):
            make(0, 0)
            return [(1, NP // BATCHES, 0), (NP // BATCHES, NP, 1)]

        block = ctx.enter_context(nc.Block())

        @block.sync
        def _(sp):
            sp.dma_start(view(area, 0, [CH, D]), x_tiles[:, 0:CH, :]).then_inc(x_first, 16)
            sp.dma_start(view(area, CH * D, [TT - CH, D]), x_tiles[:, CH:TT, :]).then_inc(x_rest, 16)
            sp.dma_start(attn32, wattn).then_inc(attn_loaded, 16)
            sp.dma_start(qv_bias[:], bias_rows[0:2 * D].unsqueeze(0)).then_inc(bias_loaded, 16)
            sp.dma_start(par[:], params).then_inc(bias_loaded, 16)
            sp.dma_start(o_bias[:], bias_rows[2 * D:3 * D].partition_broadcast(P)).then_inc(bias_loaded, 16)
            sp.dma_start(stage[:, 0:WCOLS], wexp[0]).then_inc(stage0_loaded, 16)
            sp.dma_start(stage[:, WCOLS:2 * WCOLS], wexp[1]).then_inc(stage_loaded, 16)

            def transpose_x(i, first):
                for r in range(CH):
                    t = CH * i + r
                    if not first:
                        hold(sp, xT_done[r], 16 * i)
                    hold(sp, xl_ready, t + 1)
                    sp.dma_start_transpose(xT[:, :, bass.ds(t * P, P)],
                                           xrow16[:, bass.ds(t, 1), :].rearrange("p a c -> p (a c)")
                                           ).then_inc(xT_done[r], 16)
            transpose_x(0, True)
            with sp.Fori(1, TT // CH) as i:
                transpose_x(i, False)

            sp.dma_start(out[0:TOKENS, :], x).then_inc(base_written, 16)
            sp.wait_ge(consts_ready, 1)
            sp.dma_start(out[TOKENS:TOKENS + P, :], padrow[:, 0:D]).then_inc(base_written, 16)

            def transpose_k(i, first):
                for r in range(2):
                    t = 2 * i + r
                    if not first:
                        hold(sp, kT_done[r], 16 * i)
                    hold(sp, kvl_ready, 2 * (t + 1))
                    sp.dma_start_transpose(kT[:, :, bass.ds(t * P, P)],
                                           kvrow[r][:, 0:2 * D]).then_inc(kT_done[r], 16)
            transpose_k(0, True)
            with sp.Fori(1, NP) as i:
                transpose_k(i, False)

            sp.wait_ge(scattered1, 16 * (TT + PADS))
            sp.wait_ge(scattered2, 16 * TT)
            sp.wait_ge(w_lo_pool, 2)
            sp.wait_ge(w_lo, E - 2)

            def load_x(t, r, first=False):
                if not first:
                    hold(sp, b_done, t - 3)
                sp.dma_start_transpose(
                    xg[r], slots16[bass.ds(t, 1), :, 0:2 * D].rearrange("a p c -> (a p) c")
                ).then_inc(xg_loaded[r], 16)

            def slot_step(t, r, first=False, more=True):
                r2 = r % 2
                hold(sp, hl_ready, t + 1)
                if not (first and r < 2):
                    hold(sp, y_done, t - 1)
                sp.dma_start_transpose(hT[r2], h16[r2][:, :, :].rearrange("p h i -> p (h i)")
                                       ).then_inc(hT_done[r2], 16)
                if more:
                    load_x(t + 3, (r + 3) % 4, first and r == 0)
                if not first:
                    hold(sp, y_added, 16 * (t - 3))
                sp.dma_start(meta[r], slot_tiles[:, bass.ds(t, 1), D:ROW].rearrange("p a c -> p (a c)")
                             ).then_inc(meta_loaded[r], 16)
            for r in range(3):
                load_x(r, r, True)
            for r in range(4):
                slot_step(r, r, first=True)
            with sp.Fori(1, NP) as i:
                for r in range(4):
                    slot_step(4 * i + r, r)
            for t in range(4 * NP, ST):
                slot_step(t, t % 4, more=t + 3 < ST)
            sp.wait_ge(y_added, 16 * ST)
            sp.wait_ge(fin_added, 16 * NP)

        @block.gpsimd
        def _(pool):
            g = nc.gpsimd
            g.memset(ident[:], 0.0).then_inc(pool_const, 1)
            g.memset(strict[:], 1.0).then_inc(pool_const, 1)
            g.memset(kv_mask[:], KV_SCALE / (K_SCALE * V_SCALE)).then_inc(pool_const, 1)
            g.memset(before[:], 1.0).then_inc(pool_const, 1)
            g.memset(padrow[:], 0.0).then_inc(pool_const, 1)
            g.memset(ones[:], 1.0).then_inc(pool_const, 1)
            g.iota(rev[:], pattern=[[-1, E]], base=E, channel_multiplier=0,
                   allow_small_or_imprecise_dtypes=True).then_inc(pool_const, 1)
            g.iota(step128[:], pattern=[[P, TT]], base=0, channel_multiplier=0,
                   allow_small_or_imprecise_dtypes=True).then_inc(pool_const, 1)
            g.iota(tile_no[:], pattern=[[1, ST]], base=0, channel_multiplier=0,
                   allow_small_or_imprecise_dtypes=True).then_inc(pool_const, 1)
            g.iota(pad_no[:], pattern=[[P, PADS]], base=0, channel_multiplier=1,
                   allow_small_or_imprecise_dtypes=True).then_inc(pool_const, 1)
            g.iota(xrow[:, :, D:D + 1].bitcast(I32), pattern=[[P, TT], [0, 1]], base=0,
                   channel_multiplier=1).then_inc(pool_const, 1)
            pool.wait_ge(pool_const, 11)
            g.affine_select(out=ident[:], in_=ident[:], compare_op=ALU.not_equal, fill=1.0, base=0,
                            pattern=[[-1, P]], channel_multiplier=1).then_inc(pool_const, 1)
            g.affine_select(out=strict[:], in_=strict[:], compare_op=ALU.is_gt, fill=0.0, base=0,
                            pattern=[[1, P]], channel_multiplier=-1).then_inc(pool_const, 1)
            g.affine_select(out=before[:], in_=before[:], compare_op=ALU.is_gt, fill=0.0, base=0,
                            pattern=[[1, E], [-1, E]], channel_multiplier=0).then_inc(pool_const, 1)
            blocks = kv_mask[:, :].rearrange("p (g d) -> p g d", d=HD)
            g.affine_select(out=blocks, in_=blocks, compare_op=ALU.is_ge, fill=0.0, base=0,
                            pattern=[[-HD, P // HD], [0, HD]], channel_multiplier=1).then_inc(pool_const, 1)
            g.iota(padrow[:, D:D + 1].bitcast(I32), pattern=[[0, 1]], base=TOKENS,
                   channel_multiplier=1).then_inc(pool_const, 1)
            pool.wait_ge(pool_const, 16)
            g.affine_select(out=blocks, in_=blocks, compare_op=ALU.is_ge, fill=0.0, base=HD - 1,
                            pattern=[[HD, P // HD], [0, HD]], channel_multiplier=-1).then_inc(consts_ready, 1)

            with pool.Fori(0, TT) as t:
                pool.wait_ge(xh_ready, t + 1)
                g.tensor_tensor(xrow16[:, bass.ds(t, 1), D:2 * D], xn32[:, bass.ds(t, 1), :],
                                xrow16[:, bass.ds(t, 1), 0:D], ALU.subtract).then_inc(xl_ready, 1)

            for e in range(2):
                pool.wait_ge(w_scaled, e + 1)
                g.tensor_tensor(w16[:, e, 1, :], stage[:, e * WCOLS:(e + 1) * WCOLS], w16[:, e, 0, :],
                                ALU.subtract).then_inc(w_lo_pool, 1)

            def scatter(index, row):
                return g.indirect_dma_start(slots, bass.IndirectOffsetOnAxis(ap=index, axis=0), row, None)
            pool.wait_ge(slot_ready, 3)
            pool.wait_ge(xl_ready, TT)
            pool.wait_ge(gate_ready, 2)
            for t in range(TT):
                scatter(slot[:, 0, t:t + 1], xrow[:, t, :]).then_inc(scattered1, 16)
            for c in range(PADS):
                scatter(padslot[:, c:c + 1], padrow[:]).then_inc(scattered1, 16)
            pool.wait_ge(scattered1, 16 * (TT + PADS))
            g.tensor_copy(xrow[:, :, D + 1:D + 2], gate2[:].unsqueeze(2)).then_inc(gate2_placed, 1)
            pool.wait_ge(gate2_placed, 1)
            for t in range(TT):
                scatter(slot[:, 1, t:t + 1], xrow[:, t, :]).then_inc(scattered2, 16)

            def add_expert(t, r, r2):
                hold(pool, y_ready, t + 1)
                g.indirect_dma_start(out, bass.IndirectOffsetOnAxis(ap=meta[r][:, 0:1].bitcast(I32), axis=0),
                                     ysb[r2], None, compute_op=ALU.add).then_inc(y_added, 16)
                pool.wait_ge(y_added, 16 * (t + 1))

            def add_attention(p):
                hold(pool, fin_ready, p + 1)
                g.dma_start(out_pairs[:, bass.ds(p, 1), :, :].rearrange("p a j d -> p (a j) d"), fin,
                            accum_op=ALU.add).then_inc(fin_added, 16)
                pool.wait_ge(fin_added, 16 * (p + 1))

            def step(p, b):
                for r in range(4):
                    add_expert(4 * p + r, r, r % 2)
                add_attention(p)
            pool.wait_ge(base_written, 32)
            for lo, hi, b in loops(step):
                with pool.Fori(lo, hi) as p:
                    step(p, b)
            for t in range(4 * NP, ST):
                add_expert(t, t % 4, t % 2)

        @block.scalar
        def _(act):
            a = nc.scalar
            act.wait_ge(bias_ready, 1)
            a.activation(warm[:], log_scale[:], ACT.Exp).then_inc(warm_done, 1)

            def rows(t):
                a.activation(xn32[:, bass.ds(t, 1), :].rearrange("p a d -> p (a d)"),
                             area[:, bass.ds(t * D, D)], ACT.Identity, bias=shift[:, bass.ds(t, 1)],
                             scale=rstd[:, bass.ds(t, 1)]).then_inc(xn_ready, 1)
                act.wait_ge(xn_ready, t + 1)
                a.activation(xrow16[:, bass.ds(t, 1), 0:D], xn32[:, bass.ds(t, 1), :],
                             ACT.Copy).then_inc(xh_ready, 1)
            act.wait_ge(shift_ready, 1)
            with act.Fori(0, CH) as t:
                rows(t)
            act.wait_ge(attn_loaded, 16)
            a.activation(wa16[:, 0, :], attn32, ACT.Copy, scale=SCALE).then_inc(attn_hi, 1)
            act.wait_ge(shift_ready, 2)
            with act.Fori(CH, TT) as t:
                rows(t)
            act.wait_ge(bias_ready, 3)
            a.activation(qv_bias16[:, 0, :], qv_bias[:], ACT.Copy).then_inc(bias_hi, 1)

            def hi(e):
                a.activation(w16[:, bass.ds(e, 1), 0, :].rearrange("p a c -> p (a c)"),
                             stage[:, bass.ds((e % 2) * WCOLS, WCOLS)], ACT.Copy,
                             scale=SCALE).then_inc(w_hi, 1)

            def hi_and_scaled(e):
                hi(e)
                act.wait_ge(w_hi, e + 1)
                half = stage[:, e * WCOLS:(e + 1) * WCOLS]
                a.activation(half, half, ACT.Copy, scale=SCALE).then_inc(w_scaled, 1)

            def load_expert(e):
                act.dma_start(stage[:, bass.ds((e % 2) * WCOLS, WCOLS)],
                              wexp[bass.ds(e, 1), :, :].rearrange("a p c -> (a p) c")
                              ).then_inc(stage_loaded, 16)

            act.wait_ge(stage0_loaded, 16)
            hi_and_scaled(0)
            act.wait_ge(gap_ready, 1)
            a.activation(gate2[:], gap_in[:], ACT.Exp).then_inc(gexp_ready, 1)
            act.wait_ge(stage_loaded, 16)
            hi_and_scaled(1)
            act.wait_ge(w_lo_pool, 1)
            load_expert(2)

            def heads(i, first=False, expert=False, load=False):
                for r in range(2):
                    t = 2 * i + r
                    act.wait_ge(qv_done, t + 1)
                    a.activation(eth[r][:, 0:D], ps_qv[r][:, 0:D], ACT.Exp, bias=log_scale[:, 0:1],
                                 scale=1.0 / SCALE).then_inc(exps_ready, 1)
                    a.activation(eth[r][:, D:2 * D], ps_qv[r][:, D:2 * D], ACT.Tanh, scale=0.5 / SCALE
                                 ).then_inc(exps_ready, 1)
                if expert:
                    e = i + 2
                    act.wait_ge(stage_loaded, 16 * e)
                    if load:
                        if first:
                            act.wait_ge(w_lo_pool, 2)
                        else:
                            act.wait_ge(w_lo, i)
                            act.wait_ge(w_hi, i + 1)
                        load_expert(e + 1)
                    hi(e)
                for r in range(2):
                    t = 2 * i + r
                    act.wait_ge(kv32_ready, 2 * (t + 1))
                    if not first:
                        act.wait_ge(kv_mm, t - 1)
                        act.wait_ge(kT_done[r], 16 * i)
                    a.activation(kvrow[r][:, 0:D], kv32[r][:, 0:D], ACT.Copy, bias=-SCALE
                                 ).then_inc(kvh_ready, 1)
                    a.activation(kvrow[r][:, 2 * D:3 * D], kv32[r][:, D:2 * D], ACT.Copy
                                 ).then_inc(kvh_ready, 1)

            def kv_halves(b):
                act.wait_ge(kvm_ready, 2 * (b + 1))
                a.activation(kv16[:, b, 0, :], kvm[:, :, :].rearrange("p c d -> p (c d)"), ACT.Copy
                             ).then_inc(kv_hi, 1)

            act.wait_ge(slot_ready, 3)
            heads(0, first=True, expert=True, load=True)
            with act.Fori(1, NP // 2) as i:
                heads(i, expert=True, load=True)
            kv_halves(0)
            heads(4, expert=True, load=True)
            heads(5, expert=True)
            with act.Fori(6, NP) as i:
                heads(i)
            kv_halves(1)

            def silu(t, r2):
                act.wait_ge(a_done, t + 1)
                wait(act, h_ready, t - 1)
                a.activation(s32[r2], ps_a[r2][:], ACT.Silu, scale=1.0 / SCALE).then_inc(s_ready, 1)

            def h_hi(t, r2, visit2):
                act.wait_ge(h_ready, t + 1)
                wait(act, hT_done[r2], 16 * visit2)
                a.activation(h16[r2][:, 0, :], h32[r2], ACT.Copy).then_inc(hh_ready, 1)

            def y_out(t, r, r2, visit):
                act.wait_ge(y_done, t + 1)
                act.wait_ge(meta_loaded[r], 16 * (visit + 1))
                wait(act, y_added, 16 * (t - 1))
                a.activation(ysb[r2], ps_y[r2][:, 0:D], ACT.Copy, scale=meta[r][:, 1:2]
                             ).then_inc(y_ready, 1)

            def u_gates(p):
                act.wait_ge(u_done, p + 1)
                wait(act, z_ready, p)
                for c in range(KD):
                    a.activation(uT[:, c, :], ps_c0[:, c * 2 * P:(c + 1) * 2 * P], ACT.Silu,
                                 bias=par[:, 0, c:c + 1], scale=1.0 / SCALE).then_inc(uT_ready, 1)

            def n_hi(p):
                act.wait_ge(n_ready, 2 * (p + 1))
                wait(act, nT_done, p)
                a.activation(n16[:, :, 0:D], n32, ACT.Copy).then_inc(nh_ready, 1)

            def y_norm(p):
                act.wait_ge(nT_done, p + 1)
                wait(act, z_ready, p)
                for c in range(KD):
                    a.activation(yT[:, c, :], ps_c0[:, c * 2 * P:(c + 1) * 2 * P], ACT.Identity,
                                 bias=par[:, 2, c:c + 1], scale=par[:, 1, c:c + 1]).then_inc(yT_ready, 1)

            def z_hi(p):
                act.wait_ge(z_ready, p + 1)
                wait(act, f_done, p)
                a.activation(z16[:, 0, :], z32, ACT.Copy).then_inc(zh_ready, 1)

            def step(p, b):
                t = 4 * p
                silu(t, 0)
                h_hi(t, 0, 2 * p)
                u_gates(p)
                if not (isinstance(p, int) and p == 0):
                    y_out(t - 2, 2, 0, p - 1)
                silu(t + 1, 1)
                n_hi(p)
                h_hi(t + 1, 1, 2 * p)
                if not (isinstance(p, int) and p == 0):
                    y_out(t - 1, 3, 1, p - 1)
                silu(t + 2, 0)
                h_hi(t + 2, 0, 2 * p + 1)
                y_out(t, 0, 0, p)
                y_norm(p)
                silu(t + 3, 1)
                z_hi(p)
                h_hi(t + 3, 1, 2 * p + 1)
                y_out(t + 1, 1, 1, p)
            act.wait_ge(w_lo_pool, 2)
            act.wait_ge(w_lo, E - 2)
            act.wait_ge(kT_done[0], 16 * NP)
            act.wait_ge(kT_done[1], 16 * NP)
            for lo, hi, b in loops(step):
                with act.Fori(lo, hi) as p:
                    step(p, b)
            for t in range(4 * NP, ST):
                silu(t, t % 2)
                h_hi(t, t % 2, t // 2)
                y_out(t - 2, (t - 2) % 4, t % 2, (t - 2) // 4)
            for t in range(ST - 2, ST):
                y_out(t, t % 4, t % 2, t // 4)

        @block.vector
        def _(dve):
            v = nc.vector
            v.memset(log_scale[:], math.log(SCALE) - 1.0).then_inc(bias_ready, 1)

            def rsqrt(y, var, ve, sq, eps, done, call):
                n = [RSQRT_OPS * call]

                def link(instruction):
                    n[0] = n[0] + 1
                    instruction.then_inc(done, 1)
                    dve.wait_ge(done, n[0])
                link(v.tensor_scalar(ve, var, eps, None, ALU.add))
                link(v.tensor_scalar(y.bitcast(I32), ve.bitcast(I32), -0.5, float(0x5f3759df),
                                     ALU.mult, ALU.add))
                for _ in range(NEWTON):
                    link(v.tensor_tensor(sq, y, y, ALU.mult))
                    link(v.scalar_tensor_tensor(sq, sq, -0.5, ve, ALU.mult, ALU.mult))
                    link(v.scalar_tensor_tensor(y, sq, 1.5, y, ALU.add, ALU.mult))

            def norm(t0, n, call):
                for t in range(t0, t0 + n):
                    v.bn_stats(stats[:, t, :], area[:, t * D:(t + 1) * D]).then_inc(st_done, 1)
                for t in range(t0, t0 + n):
                    dve.wait_ge(st_done, t + 1)
                    v.bn_aggr(mv[:, t, :], stats[:, t, :]).then_inc(mv_done, 1)
                dve.wait_ge(mv_done, t0 + n)
                rsqrt(rstd[:, t0:t0 + n], mv[:, t0:t0 + n, 1:2].rearrange("p t a -> p (t a)"),
                      newton[:, 0, t0:t0 + n], newton[:, 1, t0:t0 + n], EPS, rstd_done, call)
                v.scalar_tensor_tensor(shift[:, t0:t0 + n], mv[:, t0:t0 + n, 0:1].rearrange("p t a -> p (t a)"),
                                       -1.0, rstd[:, t0:t0 + n], ALU.mult, ALU.mult).then_inc(shift_ready, 1)
            dve.wait_ge(x_first, 16)
            norm(0, CH, 0)
            dve.wait_ge(x_rest, 16)
            norm(CH, TT - CH, 1)
            dve.wait_ge(attn_hi, 1)
            v.scalar_tensor_tensor(wa16[:, 1, :], attn32, SCALE, wa16[:, 0, :], ALU.mult, ALU.subtract
                                   ).then_inc(attn_lo, 1)
            dve.wait_ge(bias_loaded, 48)
            v.tensor_scalar(qv_bias[:, 0:D], qv_bias[:, 0:D], SCALE, SCALE, ALU.mult, ALU.add).then_inc(bias_ready, 1)
            v.tensor_scalar(qv_bias[:, D:2 * D], qv_bias[:, D:2 * D], SCALE, None, ALU.mult).then_inc(bias_ready, 1)
            dve.wait_ge(bias_hi, 1)
            v.tensor_tensor(qv_bias16[:, 1, :], qv_bias[:], qv_bias16[:, 0, :], ALU.subtract).then_inc(bias_lo, 1)

            def expert_lo(e):
                dve.wait_ge(w_hi, e + 1)
                v.scalar_tensor_tensor(w16[:, bass.ds(e, 1), 1, :].rearrange("p a c -> p (a c)"),
                                       stage[:, bass.ds((e % 2) * WCOLS, WCOLS)], SCALE,
                                       w16[:, bass.ds(e, 1), 0, :].rearrange("p a c -> p (a c)"),
                                       ALU.mult, ALU.subtract).then_inc(w_lo, 1)
            at = [0]

            def tmp(shape):
                n = 1
                for s in shape:
                    n *= s
                at[0] += n
                return view(area, at[0] - n, shape)
            count = [0]

            def chain(instruction):
                count[0] += 1
                instruction.then_inc(route_step, 1)
                dve.wait_ge(route_step, count[0])

            sc, sc2, pick, hit1, hit2, dest, part = [tmp([TT, E]) for _ in range(7)]
            first, second, i1, i2, gap, ge1 = [tmp([TT]) for _ in range(6)]
            slotf = tmp([TOPK, TT])
            total, tiles, base, end, rows, freed = [tmp([E]) for _ in range(6)]
            over = tmp([E, TT])
            sums = tmp([E, E])
            expf = tmp([ST, E - 1])
            expn = tmp([ST])
            padf = tmp([PADS, E])
            padn = tmp([PADS])

            def per_tile(u):
                return u.unsqueeze(2).broadcast_to([P, TT, E])

            def per_expert(u):
                return u.unsqueeze(1).broadcast_to([P, TT, E])
            dve.wait_ge(consts_ready, 1)
            dve.wait_ge(scores_done, TT // CH)
            chain(v.tensor_scalar(sc, ps_gate[:, 0:TT * E].rearrange("p (t e) -> p t e", e=E),
                                  1.0 / SCALE, None, ALU.mult))
            chain(v.tensor_reduce(first, sc, AX.X, ALU.max))
            chain(v.tensor_tensor(hit1, sc, per_tile(first), ALU.is_equal))
            chain(v.tensor_tensor(pick, hit1, per_expert(rev[:]), ALU.mult))
            chain(v.tensor_reduce(i1, pick, AX.X, ALU.max))
            chain(v.tensor_tensor(hit1, per_expert(rev[:]), per_tile(i1), ALU.is_equal))
            chain(v.scalar_tensor_tensor(sc2, hit1, -BIG, sc, ALU.mult, ALU.add))
            chain(v.tensor_reduce(second, sc2, AX.X, ALU.max))
            v.tensor_tensor(gap_in[:], second, first, ALU.subtract).then_inc(gap_ready, 1)
            chain(v.tensor_tensor(hit2, sc2, per_tile(second), ALU.is_equal))
            chain(v.tensor_tensor(pick, hit2, per_expert(rev[:]), ALU.mult))
            chain(v.tensor_reduce(i2, pick, AX.X, ALU.max))
            chain(v.tensor_tensor(hit2, per_expert(rev[:]), per_tile(i2), ALU.is_equal))
            v.tensor_tensor(m16[:], hit1, hit2, ALU.add).then_inc(mask_ready, 1)
            dve.wait_ge(gexp_ready, 1)
            chain(v.tensor_scalar(ge1, gate2[:], SCALE, SCALE, ALU.mult, ALU.add))
            chain(v.reciprocal(gap, ge1))
            v.tensor_copy(xrow[:, :, D + 1:D + 2], gap.unsqueeze(2)).then_inc(gate_ready, 1)
            v.tensor_tensor(gate2[:], gate2[:], gap, ALU.mult).then_inc(gate_ready, 1)
            dve.wait_ge(ranks_done, 1)
            chain(v.tensor_copy(total, ps_route[:, TT * E:TT * E + E]))
            chain(v.tensor_tensor(over, total.unsqueeze(2).broadcast_to([P, E, TT]),
                                  step128[:].unsqueeze(1).broadcast_to([P, E, TT]), ALU.is_gt))
            chain(v.tensor_reduce(tiles, over, AX.X, ALU.add))
            chain(v.tensor_tensor(sums, before[:], tiles.unsqueeze(1).broadcast_to([P, E, E]), ALU.mult))
            chain(v.tensor_reduce(base, sums, AX.X, ALU.add))
            chain(v.scalar_tensor_tensor(dest, per_expert(base), float(P),
                                         ps_route[:, 0:TT * E].rearrange("p (t e) -> p t e", e=E),
                                         ALU.mult, ALU.add))
            for k, hit in enumerate((hit1, hit2)):
                chain(v.tensor_tensor(part, hit, dest, ALU.mult))
                chain(v.tensor_reduce(slotf[:, k, :], part, AX.X, ALU.add))
            v.tensor_copy(slot[:], slotf).then_inc(slot_ready, 1)
            chain(v.tensor_tensor(sums, before[:], total.unsqueeze(1).broadcast_to([P, E, E]), ALU.mult))
            chain(v.tensor_reduce(rows, sums, AX.X, ALU.add))
            chain(v.scalar_tensor_tensor(freed, base, float(P), rows, ALU.mult, ALU.subtract))
            chain(v.tensor_tensor(padf, pad_no[:].unsqueeze(2).broadcast_to([P, PADS, E]),
                                  freed.unsqueeze(1).broadcast_to([P, PADS, E]), ALU.is_ge))
            chain(v.tensor_tensor(padf, padf, total.unsqueeze(1).broadcast_to([P, PADS, E]), ALU.mult))
            chain(v.tensor_reduce(padn, padf, AX.X, ALU.add))
            v.tensor_tensor(padslot[:], padn, pad_no[:], ALU.add).then_inc(slot_ready, 1)
            chain(v.tensor_tensor(end, base, tiles, ALU.add))
            chain(v.tensor_tensor(expf, end[:, 0:E - 1].unsqueeze(1).broadcast_to([P, ST, E - 1]),
                                  tile_no[:].unsqueeze(2).broadcast_to([P, ST, E - 1]), ALU.is_le))
            chain(v.tensor_reduce(expn, expf, AX.X, ALU.add))
            v.tensor_copy(tile_expert[:], expn).then_inc(slot_ready, 1)

            dve.wait_ge(slot_ready, 3)

            def heads(i, expert=False):
                for r in range(2):
                    t = 2 * i + r
                    dve.wait_ge(exps_ready, 2 * (t + 1))
                    v.scalar_tensor_tensor(kv32[r][:, 0:D], eth[r][:, 0:D], SCALE, ps_qv[r][:, 0:D],
                                           ALU.min, ALU.max).then_inc(kv32_ready, 1)
                    v.scalar_tensor_tensor(kv32[r][:, D:2 * D], eth[r][:, D:2 * D], 1.0,
                                           ps_qv[r][:, D:2 * D], ALU.add, ALU.mult).then_inc(kv32_ready, 1)
                if expert:
                    expert_lo(i + 2)
                for r in range(2):
                    t = 2 * i + r
                    dve.wait_ge(kvh_ready, 2 * (t + 1))
                    v.scalar_tensor_tensor(kvrow[r][:, D:2 * D], kv32[r][:, 0:D], -SCALE,
                                           kvrow[r][:, 0:D], ALU.add, ALU.subtract).then_inc(kvl_ready, 1)
                    v.tensor_tensor(kvrow[r][:, 3 * D:4 * D], kv32[r][:, D:2 * D],
                                    kvrow[r][:, 2 * D:3 * D], ALU.subtract).then_inc(kvl_ready, 1)

            def kv_halves(b):
                dve.wait_ge(kv_mm, TB * (b + 1))
                for c in range(KD):
                    v.tensor_tensor(kvm[:, c, :], ps_kv[c][:, 0:P], kv_mask[:], ALU.mult
                                    ).then_inc(kvm_ready, 1)
                dve.wait_ge(kv_hi, b + 1)
                v.tensor_tensor(kv16[:, b, 1, :], kvm[:, :, :].rearrange("p c d -> p (c d)"),
                                kv16[:, b, 0, :], ALU.subtract).then_inc(kv_ready, 1)

            with dve.Fori(0, NP // 2) as i:
                heads(i, expert=True)
            kv_halves(0)
            with dve.Fori(NP // 2, NP - 2) as i:
                heads(i, expert=True)
            with dve.Fori(NP - 2, NP) as i:
                heads(i)
            kv_halves(1)

            def h_mul(t, r2):
                dve.wait_ge(b_done, t + 1)
                dve.wait_ge(s_ready, t + 1)
                wait(dve, hh_ready, t - 1)
                v.scalar_tensor_tensor(h32[r2], ps_b[r2][:], 1.0 / SCALE, s32[r2],
                                       ALU.mult, ALU.mult).then_inc(h_ready, 1)

            def h_lo(t, r2):
                dve.wait_ge(hh_ready, t + 1)
                v.tensor_tensor(h16[r2][:, 1, :], h32[r2], h16[r2][:, 0, :], ALU.subtract
                                ).then_inc(hl_ready, 1)

            def center(p):
                dve.wait_ge(o_done, p + 1)
                for j in range(2):
                    v.bn_stats(stats2[:, j, :], ps_c1[:, j * D:(j + 1) * D]).then_inc(c_stats, 1)
                for j in range(2):
                    hold(dve, c_stats, 2 * p + j + 1)
                    v.bn_aggr(mv2[:, j, :], stats2[:, j, :]).then_inc(c_mv, 1)
                dve.wait_ge(c_mv, 2 * p + 2)
                rsqrt(rstd2, mv2[:, :, 1:2].rearrange("p t a -> p (t a)"), newton[:, 0, 0:2],
                      newton[:, 1, 0:2], EPS, c_rstd, p)
                for j in range(2):
                    v.tensor_scalar(n32[:, j, :], ps_c1[:, j * D:(j + 1) * D], mv2[:, j, 0:1],
                                    rstd2[:, j:j + 1], ALU.subtract, ALU.mult).then_inc(n_ready, 1)

            def n_lo(p):
                dve.wait_ge(nh_ready, p + 1)
                v.tensor_tensor(n16[:, :, D:2 * D], n32, n16[:, :, 0:D], ALU.subtract
                                ).then_inc(nl_ready, 1)

            def z_mul(p):
                dve.wait_ge(yT_ready, 2 * (p + 1))
                dve.wait_ge(uT_ready, 2 * (p + 1))
                v.tensor_tensor(z32, yT[:, :, :].rearrange("p c t -> p (c t)"),
                                uT[:, :, :].rearrange("p c t -> p (c t)"), ALU.mult).then_inc(z_ready, 1)

            def z_lo(p):
                dve.wait_ge(zh_ready, p + 1)
                v.tensor_tensor(z16[:, 1, :], z32, z16[:, 0, :], ALU.subtract).then_inc(zl_ready, 1)

            def finish(p):
                dve.wait_ge(f_done, p + 1)
                wait(dve, fin_added, 16 * p)
                v.scalar_tensor_tensor(fin, ps_c1[:, :].rearrange("p (j d) -> p j d", d=D), 1.0 / SCALE,
                                       o_bias[:].unsqueeze(1).broadcast_to([P, 2, D]),
                                       ALU.mult, ALU.add).then_inc(fin_ready, 1)

            def step(p, b):
                t = 4 * p
                h_mul(t, 0)
                h_lo(t, 0)
                center(p)
                h_mul(t + 1, 1)
                h_lo(t + 1, 1)
                n_lo(p)
                h_mul(t + 2, 0)
                h_lo(t + 2, 0)
                z_mul(p)
                h_mul(t + 3, 1)
                z_lo(p)
                h_lo(t + 3, 1)
                finish(p)
            dve.wait_ge(w_lo_pool, 2)
            dve.wait_ge(w_lo, E - 2)
            dve.wait_ge(kT_done[0], 16 * NP)
            dve.wait_ge(kT_done[1], 16 * NP)
            for lo, hi, b in loops(step):
                with dve.Fori(lo, hi) as p:
                    step(p, b)
            for t in range(4 * NP, ST):
                h_mul(t, t % 2)
                h_lo(t, t % 2)

        @block.tensor
        def _(pe):
            mm = nc.tensor.matmul
            PASSES = ((0, 0), (0, 1), (1, 0))

            pe.wait_ge(attn_lo, 1)
            with pe.Fori(0, TT // CH) as i:
                for r in range(CH):
                    pe.wait_ge(xT_done[r], 16 * (i + 1))
                    for k in range(KD):
                        for n, (w, d) in enumerate(PASSES):
                            last = mm(ps_gate[:, bass.ds((CH * i + r) * E, E)],
                                      xT[:, KD * d + k, bass.ds((CH * i + r) * P, P)],
                                      wa16[:, w, k * AC + GATE:k * AC + GATE + E],
                                      start=(k == 0 and n == 0), stop=(k == KD - 1 and n == 2))
                last.then_inc(scores_done, 1)

            pe.wait_ge(mask_ready, 1)
            mm(ps_route[:, 0:TT * E], strict[:], m16[:, :, :].rearrange("p t e -> p (t e)"),
               start=True, stop=False)
            for s in range(1, TT):
                mm(ps_route[:, s * E:TT * E], ones[:], m16[:, 0:TT - s, :].rearrange("p t e -> p (t e)"),
                   start=False, stop=(s == TT - 1))
            for s in range(TT):
                last = mm(ps_route[:, TT * E:TT * E + E], ones[:], m16[:, s, :],
                          start=(s == 0), stop=(s == TT - 1))
            last.then_inc(ranks_done, 1)

            def qv(t, r):
                wait(pe, kv32_ready, 2 * (t - 1))
                for n in range(2):
                    mm(ps_qv[r][:], ones[0:1, :], qv_bias16[:, n, :], start=(n == 0), stop=False)
                for k in range(KD):
                    for n, (w, d) in enumerate(PASSES):
                        last = mm(ps_qv[r][:], xT[:, KD * d + k, bass.ds(t * P, P)],
                                  wa16[:, w, k * AC + WQ:k * AC + WQ + 2 * D], start=False, stop=(k == KD - 1 and n == 2))
                last.then_inc(qv_done, 1)

            def kv(t, r, start, stop):
                pe.wait_ge(kvl_ready, 2 * (t + 1))
                for c in range(KD):
                    for n, (w, d) in enumerate(PASSES):
                        last = mm(ps_kv[c][:, 0:P], kvrow[r][:, w * D + c * P:w * D + (c + 1) * P],
                                  kvrow[r][:, (2 + d) * D + c * P:(2 + d) * D + (c + 1) * P],
                                  start=(start and n == 0), stop=(stop and n == 2), skip_group_check=True)
                last.then_inc(kv_mm, 1)

            pe.wait_ge(bias_lo, 1)

            def batch(b):
                i0 = b * NP // 2
                qv(2 * i0, 0)
                qv(2 * i0 + 1, 1)
                if b > 0:
                    pe.wait_ge(kvm_ready, 2 * b)
                kv(2 * i0, 0, True, False)
                with pe.Fori(i0 + 1, i0 + NP // 2) as i:
                    qv(2 * i, 0)
                    kv(2 * i - 1, 1, False, False)
                    qv(2 * i + 1, 1)
                    kv(2 * i, 0, False, False)
                kv(2 * (i0 + NP // 2) - 1, 1, False, True)
            batch(0)
            batch(1)

            def expert_of(t):
                return pe.value_load(tile_expert[0:1, bass.ds(t, 1)], min_val=0, max_val=E - 1)

            def hidden(t, r, r2, visit):
                e = expert_of(t)
                pe.wait_ge(xg_loaded[r], 16 * (visit + 1))
                for bank_, col, done, taken in ((ps_a[r2], W1, a_done, s_ready), (ps_b[r2], W3, b_done, h_ready)):
                    wait(pe, taken, t - 1)
                    for k in range(KD):
                        at = col + k * I
                        for n, (w, d) in enumerate(PASSES):
                            last = mm(bank_[:], xg[r][:, KD * d + k, :],
                                      w16[:, bass.ds(e, 1), w, at:at + I].rearrange("p a c -> p (a c)"),
                                      start=(k == 0 and n == 0), stop=(k == KD - 1 and n == 2))
                    last.then_inc(done, 1)

            def down(t, r2, visit2):
                e = expert_of(t)
                pe.wait_ge(hT_done[r2], 16 * (visit2 + 1))
                wait(pe, y_ready, t - 1)
                for c in range(IC):
                    at = W2 + c * D
                    for n, (w, d) in enumerate(PASSES):
                        last = mm(ps_y[r2][:, 0:D], hT[r2][:, IC * d + c, :],
                                  w16[:, bass.ds(e, 1), w, at:at + D].rearrange("p a c -> p (a c)"),
                                  start=(c == 0 and n == 0), stop=(c == IC - 1 and n == 2))
                last.then_inc(y_done, 1)

            def u_proj(p):
                wait(pe, yT_ready, 2 * p)
                for c in range(KD):
                    for k in range(KD):
                        at = k * AC + WU + c * P
                        for n, (w, d) in enumerate(PASSES):
                            last = mm(ps_c0[:, c * 2 * P:(c + 1) * 2 * P], wa16[:, w, at:at + P],
                                      xT[:, KD * d + k, bass.ds(p * 2 * P, 2 * P)],
                                      start=(k == 0 and n == 0), stop=(k == KD - 1 and n == 2))
                last.then_inc(u_done, 1)

            def q_kv(p, b):
                wait(pe, fin_ready, p)
                for j in range(2):
                    for c in range(KD):
                        for n, (w, d) in enumerate(PASSES):
                            last = mm(ps_c1[:, j * D + c * P:j * D + (c + 1) * P],
                                      kT[:, KD * d + c, bass.ds((2 * p + j) * P, P)],
                                      kv16[:, b, w, c * P:(c + 1) * P],
                                      start=(n == 0), stop=(n == 2))
                last.then_inc(o_done, 1)

            def turn(p):
                pe.wait_ge(nl_ready, p + 1)
                pe.wait_ge(uT_ready, 2 * (p + 1))
                for c in range(KD):
                    for j in range(2):
                        for w in range(2):
                            last = mm(ps_c0[:, c * 2 * P + j * P:c * 2 * P + (j + 1) * P],
                                      n16[:, j, w * D + c * P:w * D + (c + 1) * P], ident[:],
                                      start=(w == 0), stop=(w == 1))
                last.then_inc(nT_done, 1)

            def project(p):
                pe.wait_ge(zl_ready, p + 1)
                for j in range(2):
                    for c in range(KD):
                        at = c * AC + WO
                        for n, (w, d) in enumerate(PASSES):
                            last = mm(ps_c1[:, j * D:(j + 1) * D],
                                      z16[:, d, c * 2 * P + j * P:c * 2 * P + (j + 1) * P],
                                      wa16[:, w, at:at + D],
                                      start=(c == 0 and n == 0), stop=(c == KD - 1 and n == 2))
                last.then_inc(f_done, 1)

            def step(p, b):
                t = 4 * p
                rest = not (isinstance(p, int) and p == 0)
                hidden(t, 0, 0, p)
                u_proj(p)
                if rest:
                    down(t - 2, 0, 2 * p - 1)
                q_kv(p, b)
                hidden(t + 1, 1, 1, p)
                if rest:
                    down(t - 1, 1, 2 * p - 1)
                hidden(t + 2, 2, 0, p)
                down(t, 0, 2 * p)
                turn(p)
                hidden(t + 3, 3, 1, p)
                down(t + 1, 1, 2 * p)
                project(p)
            pe.wait_ge(slot_ready, 3)
            pe.wait_ge(w_lo_pool, 2)
            pe.wait_ge(w_lo, E - 2)
            pe.wait_ge(kv_ready, BATCHES)
            pe.wait_ge(kT_done[0], 16 * NP)
            pe.wait_ge(kT_done[1], 16 * NP)
            for lo, hi, b in loops(step):
                with pe.Fori(lo, hi) as p:
                    step(p, b)
            for t in range(4 * NP, ST):
                hidden(t, t % 4, t % 2, t // 4)
                down(t - 2, t % 2, (t - 2) // 2)
            for t in range(ST - 2, ST):
                down(t, t % 2, t // 2)


def kernel(**inputs):
    import numpy as np
    import concourse.bacc as bacc
    from concourse.bass_utils import run_bass_kernel_spmd

    def get(name):
        return np.ascontiguousarray(inputs["L0_" + name])

    x = get("attn_x")
    shape = x.shape
    rows = [get("ffn_gate_w").T, get("attn_Wu"), get("attn_Wqk"), get("attn_Wv"), get("attn_Wo")]
    wattn = np.concatenate(rows, axis=1).reshape(KD, P, AC).transpose(1, 0, 2).reshape(P, KD * AC)

    def chunks(w):
        e, k, m = w.shape
        return w.reshape(e, k // P, P, m).transpose(0, 2, 1, 3).reshape(e, P, k // P * m)
    wexp = np.concatenate([chunks(get("ffn_w1").transpose(0, 2, 1)), chunks(get("ffn_w3").transpose(0, 2, 1)),
                           chunks(get("ffn_w2").transpose(0, 2, 1))], axis=2)
    params = np.stack([get(n).reshape(KD, P).T for n in ("attn_bu", "attn_ln_g", "attn_ln_b")], axis=1)
    bias_rows = np.concatenate([get("attn_bqk"), get("attn_bv"), get("attn_bo")])
    arrays = {"x": x.reshape(TOKENS, D), "wattn": wattn, "wexp": wexp, "params": params,
              "bias_rows": bias_rows}
    arrays = {n: np.ascontiguousarray(a) for n, a in arrays.items()}

    nc = bacc.Bacc("TRN2", target_bir_lowering=False, num_devices=1)
    args = [nc.dram_tensor(n, a.shape, mybir.dt.from_np(a.dtype), kind="ExternalInput").ap()
            for n, a in arrays.items()]
    out = nc.dram_tensor("out", (TOKENS + P, D), F32, kind="ExternalOutput").ap()
    build(nc, *args, out)
    r = run_bass_kernel_spmd(nc, [arrays], core_ids=[0])
    return r.results[0]["out"][0:TOKENS].reshape(shape)
```

```python
import math
from contextlib import ExitStack

import concourse.bass as bass
from concourse import mybir

F32 = mybir.dt.float32
F16 = mybir.dt.float16
I32 = mybir.dt.int32
ALU = mybir.AluOpType
ACT = mybir.ActivationFunctionType
AX = mybir.AxisListType

P = 128
D = 256
KD = D // P
TOKENS = 2048
BATCHES = 2
TT = TOKENS // P
TB = TT // BATCHES
NP = TT // 2
HD = 16
E = 8
I = 512
IC = I // P
TOPK = 2
ST = TOPK * TOKENS // P + E - 1
PADS = ST - TOPK * TOKENS // P
WCOLS = 2 * KD * I + IC * D
W1, W3, W2 = 0, KD * I, 2 * KD * I
ROW = D + 2
AC = E + 4 * D
GATE, WU, WQ, WO = 0, E, E + D, E + 3 * D
SCALE = 64.0
K_SCALE = SCALE
V_SCALE = 2.0 * SCALE
KV_SCALE = 1.0 / K_SCALE
EPS = 1e-5
BIG = 1e30
CH = 4
NEWTON = 3
RSQRT_OPS = 2 + 3 * NEWTON


def build(nc, x, wattn, wexp, params, bias_rows, out):
    ctx = ExitStack()
    with ctx:
        def sb(name, shape, dt=F32):
            return ctx.enter_context(nc.sbuf_tensor(name, shape, dt))

        def psum(name):
            return ctx.enter_context(nc.psum_tensor(name, [P, 512], F32))

        def sem(name):
            return ctx.enter_context(nc.semaphore(name))

        def view(base, start, shape, dt=F32):
            n = 1
            for s in shape:
                n *= s
            words = n if dt != F16 else n // 2
            v = base[:, start:start + words]
            if dt != F32:
                v = v.bitcast(dt)
            if len(shape) == 2:
                v = v.rearrange("p (a b) -> p a b", b=shape[1])
            if len(shape) == 3:
                v = v.rearrange("p (a b c) -> p a b c", b=shape[1], c=shape[2])
            return v

        regions = sb("regions", [P, (E + 2) * WCOLS])
        w16 = regions[:, 0:E * WCOLS].bitcast(F16).rearrange("p (e h c) -> p e h c", e=E, h=2)
        attn32 = view(regions, 9 * WCOLS, [KD * AC])
        wa16 = sb("wa16", [P, 2, KD * AC], F16)
        area = sb("area", [P, TT * D])
        xrow = sb("xrow", [P, TT, ROW])
        xT = sb("xT", [P, TT, 2 * KD, P], F16)
        uT = xT[:, :, :, :].rearrange("p t c i -> p (t c i)").bitcast(F32)
        kT = sb("kT", [P, TT, 2 * KD, P], F16)
        xn32 = kT[:, :, :, :].rearrange("p t c i -> p (t c i)").bitcast(F32).rearrange("p (t d) -> p t d", d=D)
        padrow = sb("padrow", [P, ROW])
        qv_bias = sb("qv_bias", [2, 2 * D])
        qv_bias32 = sb("qv_bias32", [2, 2 * D])
        qv_bias16 = sb("qv_bias16", [2, 2 * D], F16)
        row_no = sb("row_no", [2, 1])
        o_bias = sb("o_bias", [P, D])
        par = sb("par", [P, 3, KD])
        ident = sb("ident", [P, P], F16)
        strict = sb("strict", [P, P], F16)
        ones = sb("ones", [P, P], F16)
        kv_mask = sb("kv_mask", [P, P])
        rev = sb("rev", [P, E])
        before = sb("before", [P, E, E])
        step128 = sb("step128", [P, TT])
        tile_no = sb("tile_no", [P, ST])
        pad_no = sb("pad_no", [P, PADS])
        stats = sb("stats", [P, TT, 6])
        mv = sb("mv", [P, TT, 2])
        rstd = sb("rstd", [P, TT])
        m16 = sb("m16", [P, TT, E], F16)
        slot = sb("slot", [P, TOPK, TT], I32)
        gap_in = sb("gap_in", [P, TT])
        gate2 = sb("gate2", [P, TT])
        warm = sb("warm", [P, 1])
        padslot = sb("padslot", [P, PADS], I32)
        tile_expert = sb("tile_expert", [P, ST], I32)
        kv16 = sb("kv16", [P, BATCHES, 2, KD * P], F16)
        kvm = sb("kvm", [P, KD, P])
        log_scale = sb("log_scale", [P, 1])
        newton = sb("newton", [P, 2, TT])
        shift = sb("shift", [P, TT])
        kv32 = [view(area, 512 * r, [2 * D]) for r in range(CH)]
        krow = view(area, 2048, [CH, 2 * D], F16)
        n32 = view(area, 512, [2, D])
        n16 = view(area, 1024, [2, 2 * D], F16)
        yT = view(area, 1536, [KD, 2 * P])
        z32 = view(area, 2048, [KD * 2 * P])
        z16 = view(area, 2560, [2, KD * 2 * P], F16)
        fin = view(area, 3072, [2, D])
        stats2 = view(area, 3584, [2, 6])
        mv2 = view(area, 3600, [2, 2])
        rstd2 = view(area, 3608, [2])
        stage = regions[:, E * WCOLS:(E + 2) * WCOLS]
        xg = [view(stage, 256 * r, [2 * KD, P], F16) for r in range(4)]
        meta = [view(stage, 1024 + 4 * r, [2]) for r in range(4)]
        s32 = [view(stage, 1040 + 512 * r, [I]) for r in range(2)]
        h32 = [view(stage, 2064 + 512 * r, [I]) for r in range(2)]
        h16 = [view(stage, 3088 + 512 * r, [2, I], F16) for r in range(2)]
        ysb = [view(stage, 4112 + 256 * r, [D]) for r in range(2)]
        hT = [view(stage, 4624 + 512 * r, [2 * IC, P], F16) for r in range(2)]

        bank = [psum(f"bank{i}") for i in range(8)]
        ps_gate, ps_route = bank[0], bank[1]
        ps_qv, ps_kv = bank[2:4] + bank[6:8], bank[4:6]
        ps_x, ps_u = ps_qv, bank[0:2]
        ps_a, ps_b = bank[0:2], bank[2:4]
        ps_y = bank[4:6]
        ps_c0, ps_c1 = bank[6], bank[7]

        slots = nc.dram_tensor("slots", [ST * P, ROW], F32, kind="Internal").ap()

        x_first = sem("x_first")
        x_rest = sem("x_rest")
        attn_loaded = sem("attn_loaded")
        bias_loaded = sem("bias_loaded")
        raw_loaded = [sem(f"raw_loaded{e}") for e in range(E)]
        pool_const = sem("pool_const")
        consts_ready = sem("consts_ready")
        log_scale_set = sem("log_scale_set")
        qv_bias_loaded = sem("qv_bias_loaded")
        bias_hi = sem("bias_hi")
        bias_scaled = sem("bias_scaled")
        bias_lo = sem("bias_lo")
        warm_done = sem("warm_done")
        attn_hi = sem("attn_hi")
        attn_lo = sem("attn_lo")
        w_hi = sem("w_hi")
        w_scaled = sem("w_scaled")
        w_lo_pool = sem("w_lo_pool")
        w_lo = sem("w_lo")
        shift_ready = sem("shift_ready")
        st_done = sem("st_done")
        mv_done = sem("mv_done")
        rstd_done = sem("rstd_done")
        xn_ready = sem("xn_ready")
        xh_ready = sem("xh_ready")
        xl_ready = sem("xl_ready")
        x_turned = sem("x_turned")
        xT_act = sem("xT_act")
        xT_dve = sem("xT_dve")
        scores_done = sem("scores_done")
        route_step = sem("route_step")
        gap_ready = sem("gap_ready")
        gexp_ready = sem("gexp_ready")
        mask_ready = sem("mask_ready")
        ranks_done = sem("ranks_done")
        gate_ready = sem("gate_ready")
        slot_ready = sem("slot_ready")
        scattered1 = [sem(f"scattered1_{g}") for g in range(TT // CH)]
        pads_scattered = sem("pads_scattered")
        gate2_placed = sem("gate2_placed")
        scattered2 = sem("scattered2")
        base_written = sem("base_written")
        qv_done = sem("qv_done")
        exps_ready = sem("exps_ready")
        kv32_ready = sem("kv32_ready")
        kh_ready = sem("kh_ready")
        kl_ready = sem("kl_ready")
        kT_done = sem("kT_done")
        kv_mm = sem("kv_mm")
        kvm_ready = sem("kvm_ready")
        kv_hi = sem("kv_hi")
        kv_ready = sem("kv_ready")
        xg_loaded = [sem(f"xg_loaded{r}") for r in range(4)]
        meta_loaded = [sem(f"meta_loaded{r}") for r in range(4)]
        hT_done = [sem(f"hT_done{r}") for r in range(2)]
        a_done = sem("a_done")
        b_done = sem("b_done")
        s_ready = sem("s_ready")
        h_ready = sem("h_ready")
        hh_ready = sem("hh_ready")
        hl_ready = sem("hl_ready")
        y_done = sem("y_done")
        y_ready = sem("y_ready")
        y_added = sem("y_added")
        u_done = sem("u_done")
        uT_ready = sem("uT_ready")
        gates_ready = sem("gates_ready")
        o_done = sem("o_done")
        c_stats = sem("c_stats")
        c_mv = sem("c_mv")
        c_rstd = sem("c_rstd")
        n_ready = sem("n_ready")
        nh_ready = sem("nh_ready")
        nl_ready = sem("nl_ready")
        nT_done = sem("nT_done")
        yT_ready = sem("yT_ready")
        z_ready = sem("z_ready")
        zh_ready = sem("zh_ready")
        zl_ready = sem("zl_ready")
        f_done = sem("f_done")
        fin_ready = sem("fin_ready")
        fin_added = sem("fin_added")
        held = sem("held")

        def wait(eng, semaphore, value):
            if not (isinstance(value, int) and value <= 0):
                eng.wait_ge(semaphore, value)

        def hold(eng, semaphore, value):
            eng.wait_ge(semaphore, value)
            eng.sem_inc(held, 1)

        x_tiles = x.rearrange("(t p) d -> p t d", p=P)
        out_pairs = out[0:TOKENS, :].rearrange("(i j p) d -> p i j d", j=2, p=P)
        slot_tiles = slots.rearrange("(s p) c -> p s c", p=P)
        slots16 = slots.bitcast(F16).rearrange("(s p) c -> s p c", p=P)
        xrow16 = xrow[:, :, 0:D].bitcast(F16)

        def loops(make):
            make(0, 0)
            return [(1, NP // BATCHES, 0), (NP // BATCHES, NP, 1)]

        block = ctx.enter_context(nc.Block())

        @block.sync
        def _(sp):
            sp.dma_start(view(area, 0, [CH, D]), x_tiles[:, 0:CH, :]).then_inc(x_first, 16)
            sp.dma_start(qv_bias[:], bias_rows[0:2 * D].partition_broadcast(2)).then_inc(qv_bias_loaded, 16)
            sp.dma_start(view(area, CH * D, [TT - CH, D]), x_tiles[:, CH:TT, :]).then_inc(x_rest, 16)
            sp.dma_start(attn32, wattn).then_inc(attn_loaded, 16)
            sp.dma_start(par[:], params).then_inc(bias_loaded, 16)
            sp.dma_start(o_bias[:], bias_rows[2 * D:3 * D].partition_broadcast(P)).then_inc(bias_loaded, 16)
            def load_expert(e):
                sp.dma_start(regions[:, (e + 2) * WCOLS:(e + 3) * WCOLS], wexp[e]).then_inc(raw_loaded[e], 16)
            for e in range(E - 1):
                load_expert(e)
            sp.wait_ge(attn_lo, 1 + KD)
            load_expert(E - 1)
            def transpose_k(g):
                sp.wait_ge(kl_ready, CH * (g + 1))
                sp.dma_start_transpose(kT[:, CH * g:CH * (g + 1), :, :].rearrange("p t c i -> p (t c) i"),
                                       krow[:, :, :].rearrange("p t d -> p (t d)")).then_inc(kT_done, 16)
            transpose_k(0)
            sp.dma_start(out[0:TOKENS, :], x).then_inc(base_written, 16)
            sp.wait_ge(consts_ready, 1)
            sp.dma_start(out[TOKENS:TOKENS + P, :], padrow[:, 0:D]).then_inc(base_written, 16)
            transpose_k(1)
            transpose_k(2)

            for g in range(TT // CH):
                sp.wait_ge(scattered1[g], 16 * CH)
            sp.wait_ge(pads_scattered, 16 * PADS)
            sp.wait_ge(scattered2, 16 * TT)
            sp.wait_ge(w_lo, E - 2)

            def load_x(t, r, first=False):
                if not first:
                    hold(sp, b_done, t - 3)
                sp.dma_start_transpose(
                    xg[r], slots16[bass.ds(t, 1), :, 0:2 * D].rearrange("a p c -> (a p) c")
                ).then_inc(xg_loaded[r], 16)

            def slot_step(t, r, first=False, more=True):
                r2 = r % 2
                hold(sp, hl_ready, t + 1)
                if not (first and r < 2):
                    hold(sp, y_done, t - 1)
                sp.dma_start_transpose(hT[r2], h16[r2][:, :, :].rearrange("p h i -> p (h i)")
                                       ).then_inc(hT_done[r2], 16)
                if more:
                    load_x(t + 3, (r + 3) % 4, first and r == 0)
                if not first:
                    hold(sp, y_added, 16 * (t - 3))
                sp.dma_start(meta[r], slot_tiles[:, bass.ds(t, 1), D:ROW].rearrange("p a c -> p (a c)")
                             ).then_inc(meta_loaded[r], 16)
            load_x(0, 0, True)
            transpose_k(3)
            load_x(1, 1, True)
            load_x(2, 2, True)
            for r in range(4):
                slot_step(r, r, first=True)
            with sp.Fori(1, NP) as i:
                for r in range(4):
                    slot_step(4 * i + r, r)
            for t in range(4 * NP, ST):
                slot_step(t, t % 4, more=t + 3 < ST)
            sp.wait_ge(y_added, 16 * ST)
            sp.wait_ge(fin_added, 16 * NP)

        @block.gpsimd
        def _(pool):
            g = nc.gpsimd
            g.memset(ident[:], 0.0).then_inc(pool_const, 1)
            g.memset(strict[:], 1.0).then_inc(pool_const, 1)
            g.memset(kv_mask[:], KV_SCALE / (K_SCALE * V_SCALE)).then_inc(pool_const, 1)
            g.memset(before[:], 1.0).then_inc(pool_const, 1)
            g.memset(padrow[:], 0.0).then_inc(pool_const, 1)
            g.memset(ones[:], 1.0).then_inc(pool_const, 1)
            g.iota(rev[:], pattern=[[-1, E]], base=E, channel_multiplier=0,
                   allow_small_or_imprecise_dtypes=True).then_inc(pool_const, 1)
            g.iota(step128[:], pattern=[[P, TT]], base=0, channel_multiplier=0,
                   allow_small_or_imprecise_dtypes=True).then_inc(pool_const, 1)
            g.iota(tile_no[:], pattern=[[1, ST]], base=0, channel_multiplier=0,
                   allow_small_or_imprecise_dtypes=True).then_inc(pool_const, 1)
            g.iota(pad_no[:], pattern=[[P, PADS]], base=0, channel_multiplier=1,
                   allow_small_or_imprecise_dtypes=True).then_inc(pool_const, 1)
            g.iota(xrow[:, :, D:D + 1].bitcast(I32), pattern=[[P, TT], [0, 1]], base=0,
                   channel_multiplier=1).then_inc(pool_const, 1)
            g.iota(row_no[:], pattern=[[0, 1]], base=0, channel_multiplier=1,
                   allow_small_or_imprecise_dtypes=True).then_inc(pool_const, 1)
            pool.wait_ge(pool_const, 12)
            g.affine_select(out=ident[:], in_=ident[:], compare_op=ALU.not_equal, fill=1.0, base=0,
                            pattern=[[-1, P]], channel_multiplier=1).then_inc(pool_const, 1)
            g.affine_select(out=strict[:], in_=strict[:], compare_op=ALU.is_gt, fill=0.0, base=0,
                            pattern=[[1, P]], channel_multiplier=-1).then_inc(pool_const, 1)
            g.affine_select(out=before[:], in_=before[:], compare_op=ALU.is_gt, fill=0.0, base=0,
                            pattern=[[1, E], [-1, E]], channel_multiplier=0).then_inc(pool_const, 1)
            blocks = kv_mask[:, :].rearrange("p (g d) -> p g d", d=HD)
            g.affine_select(out=blocks, in_=blocks, compare_op=ALU.is_ge, fill=0.0, base=0,
                            pattern=[[-HD, P // HD], [0, HD]], channel_multiplier=1).then_inc(pool_const, 1)
            g.iota(padrow[:, D:D + 1].bitcast(I32), pattern=[[0, 1]], base=TOKENS,
                   channel_multiplier=1).then_inc(pool_const, 1)
            pool.wait_ge(pool_const, 17)
            g.affine_select(out=blocks, in_=blocks, compare_op=ALU.is_ge, fill=0.0, base=HD - 1,
                            pattern=[[HD, P // HD], [0, HD]], channel_multiplier=-1).then_inc(consts_ready, 1)

            pool.wait_ge(qv_bias_loaded, 16)
            g.tensor_scalar(qv_bias[:, 0:D], qv_bias[:, 0:D], SCALE, SCALE, ALU.mult, ALU.add
                            ).then_inc(bias_scaled, 1)
            g.tensor_scalar(qv_bias[:, D:2 * D], qv_bias[:, D:2 * D], SCALE, None, ALU.mult
                            ).then_inc(bias_scaled, 1)
            for t in range(TT):
                pool.wait_ge(xh_ready, t + 1)
                g.tensor_tensor(xrow16[:, t, D:2 * D], xn32[:, t, :], xrow16[:, t, 0:D],
                                ALU.subtract).then_inc(xl_ready, 1)

            pool.wait_ge(bias_hi, 1)
            g.tensor_scalar(qv_bias32[:], qv_bias16[:], row_no[:, 0:1], None, ALU.mult).then_inc(bias_lo, 1)
            pool.wait_ge(bias_lo, 1)
            g.tensor_tensor(qv_bias16[:], qv_bias[:], qv_bias32[:], ALU.subtract).then_inc(bias_lo, 1)

            for n in range(2):
                part = slice(n * WCOLS // 2, (n + 1) * WCOLS // 2)
                pool.wait_ge(w_scaled, n + 1)
                g.tensor_tensor(w16[:, 0, 1, part], regions[:, 2 * WCOLS:3 * WCOLS][:, part],
                                w16[:, 0, 0, part], ALU.subtract).then_inc(w_lo_pool, 1)

            def scatter(index, row):
                return g.indirect_dma_start(slots, bass.IndirectOffsetOnAxis(ap=index, axis=0), row, None)
            pool.wait_ge(slot_ready, 1)
            pool.wait_ge(xl_ready, TT)
            pool.wait_ge(gate_ready, 2)
            for t in range(TT):
                scatter(slot[:, 0, t:t + 1], xrow[:, t, :]).then_inc(scattered1[t // CH], 16)
            pool.wait_ge(slot_ready, 2)
            for c in range(PADS):
                scatter(padslot[:, c:c + 1], padrow[:]).then_inc(pads_scattered, 16)
            for c in range(TT // CH):
                pool.wait_ge(scattered1[c], 16 * CH)
                g.tensor_copy(xrow[:, CH * c:CH * (c + 1), D + 1:D + 2],
                              gate2[:, CH * c:CH * (c + 1)].unsqueeze(2)).then_inc(gate2_placed, 1)
                pool.wait_ge(gate2_placed, c + 1)
                for t in range(CH * c, CH * (c + 1)):
                    scatter(slot[:, 1, t:t + 1], xrow[:, t, :]).then_inc(scattered2, 16)

            def add_expert(t, r, r2):
                hold(pool, y_ready, t + 1)
                g.indirect_dma_start(out, bass.IndirectOffsetOnAxis(ap=meta[r][:, 0:1].bitcast(I32), axis=0),
                                     ysb[r2], None, compute_op=ALU.add).then_inc(y_added, 16)
                pool.wait_ge(y_added, 16 * (t + 1))

            def add_attention(p):
                hold(pool, fin_ready, p + 1)
                g.dma_start(out_pairs[:, bass.ds(p, 1), :, :].rearrange("p a j d -> p (a j) d"), fin,
                            accum_op=ALU.add).then_inc(fin_added, 16)
                pool.wait_ge(fin_added, 16 * (p + 1))

            def step(p, b):
                for r in range(4):
                    add_expert(4 * p + r, r, r % 2)
                add_attention(p)
            pool.wait_ge(base_written, 32)
            for lo, hi, b in loops(step):
                with pool.Fori(lo, hi) as p:
                    step(p, b)
            for t in range(4 * NP, ST):
                add_expert(t, t % 4, t % 2)

        @block.scalar
        def _(act):
            a = nc.scalar
            act.wait_ge(log_scale_set, 1)
            a.activation(warm[:], log_scale[:], ACT.Exp).then_inc(warm_done, 1)

            act.wait_ge(bias_scaled, 2)
            a.activation(qv_bias16[:], qv_bias[:], ACT.Copy).then_inc(bias_hi, 1)

            def x_hi(t):
                act.wait_ge(xn_ready, t + 1)
                a.activation(xrow16[:, t, 0:D], xn32[:, t, :], ACT.Copy).then_inc(xh_ready, 1)

            def xT_out(t):
                act.wait_ge(x_turned, t + 1)
                a.activation(xT[:, t, :, :].rearrange("p c i -> p (c i)"), ps_x[t % CH][:],
                             ACT.Copy).then_inc(xT_act, 1)
            for t in range(CH):
                x_hi(t)
            for t in range(CH):
                xT_out(t)
            act.wait_ge(attn_loaded, 16)
            a.activation(wa16[:, 0, :], attn32, ACT.Copy, scale=SCALE).then_inc(attn_hi, 1)
            x_hi(CH)
            x_hi(CH + 1)
            x_hi(CH + 2)
            for t in range(CH, TT, 2):
                for more in (t + 3, t + 4):
                    if more < TT:
                        x_hi(more)
                xT_out(t)
            def raw(e):
                return regions[:, (e + 2) * WCOLS:(e + 3) * WCOLS]

            def hi(e):
                act.wait_ge(raw_loaded[e], 16)
                a.activation(w16[:, e, 0, :], raw(e), ACT.Copy, scale=SCALE).then_inc(w_hi, 1)

            hi(0)
            act.wait_ge(w_hi, 1)
            for n in range(2):
                part = raw(0)[:, n * WCOLS // 2:(n + 1) * WCOLS // 2]
                a.activation(part, part, ACT.Copy, scale=SCALE).then_inc(w_scaled, 1)
            act.wait_ge(gap_ready, 1)
            a.activation(gate2[:], gap_in[:], ACT.Exp, scale=1.0 / SCALE).then_inc(gexp_ready, 1)
            hi(1)

            def exps(i, first=False, tiles=range(CH)):
                for r in tiles:
                    t = CH * i + r
                    act.wait_ge(qv_done, t + 1)
                    if not first:
                        act.wait_ge(kl_ready, t + 1 - CH)
                        act.wait_ge(kv_mm, t + 1 - CH)
                    a.activation(kv32[r][:, 0:D], ps_qv[r][:, 0:D], ACT.Exp, bias=log_scale[:, 0:1],
                                 scale=1.0 / SCALE).then_inc(exps_ready, 1)
                    a.activation(kv32[r][:, D:2 * D], ps_qv[r][:, D:2 * D], ACT.Tanh, scale=0.5 / SCALE
                                 ).then_inc(exps_ready, 1)

            def halves(i, first=False):
                if not first:
                    act.wait_ge(kT_done, 16 * i)
                for r in range(CH):
                    t = CH * i + r
                    act.wait_ge(kv32_ready, 2 * (t + 1))
                    a.activation(krow[:, r, 0:D], kv32[r][:, 0:D], ACT.Copy, bias=-SCALE
                                 ).then_inc(kh_ready, 1)
                    a.activation(kv32[r][:, 0:D], kv32[r][:, 0:D], ACT.Copy, bias=-SCALE
                                 ).then_inc(kh_ready, 1)

            def kv_halves(b):
                act.wait_ge(kvm_ready, 2 * (b + 1))
                a.activation(kv16[:, b, 0, :], kvm[:, :, :].rearrange("p c d -> p (c d)"), ACT.Copy
                             ).then_inc(kv_hi, 1)

            def u_out(p):
                act.wait_ge(u_done, p + 1)
                if p == 0:
                    act.wait_ge(bias_loaded, 32)
                for c in range(KD):
                    a.activation(uT[:, (p * KD + c) * 2 * P:(p * KD + c + 1) * 2 * P],
                                 ps_u[p % 2][:, c * 2 * P:(c + 1) * 2 * P], ACT.Identity,
                                 bias=par[:, 0, c:c + 1], scale=1.0 / SCALE).then_inc(uT_ready, 1)

            exps(0, first=True, tiles=range(CH - 1))
            act.wait_ge(w_lo_pool, 2)
            hi(2)
            exps(0, first=True, tiles=range(CH - 1, CH))
            halves(0, first=True)
            act.wait_ge(w_lo, 1)
            hi(3)
            exps(1)
            act.wait_ge(w_lo, 2)
            hi(4)
            halves(1)
            u_out(0)
            u_out(1)
            act.wait_ge(w_lo, 3)
            hi(5)
            exps(2)
            halves(2)
            kv_halves(0)
            act.wait_ge(w_lo, 4)
            hi(6)
            exps(3)
            u_out(2)
            u_out(3)
            act.wait_ge(w_lo, 5)
            hi(7)
            halves(3)
            for p in range(NP // 2, NP):
                u_out(p)
            a.activation(warm[:], log_scale[:], ACT.Silu).then_inc(warm_done, 1)
            kv_halves(1)

            def silu(t, r2):
                act.wait_ge(a_done, t + 1)
                wait(act, h_ready, t - 1)
                a.activation(s32[r2], ps_a[r2][:], ACT.Silu, scale=1.0 / SCALE).then_inc(s_ready, 1)

            def h_hi(t, r2, visit2):
                act.wait_ge(h_ready, t + 1)
                wait(act, hT_done[r2], 16 * visit2)
                a.activation(h16[r2][:, 0, :], h32[r2], ACT.Copy).then_inc(hh_ready, 1)

            def y_out(t, r, r2, visit):
                act.wait_ge(y_done, t + 1)
                act.wait_ge(meta_loaded[r], 16 * (visit + 1))
                wait(act, y_added, 16 * (t - 1))
                a.activation(ysb[r2], ps_y[r2][:, 0:D], ACT.Copy, scale=meta[r][:, 1:2]
                             ).then_inc(y_ready, 1)

            def u_gates(p):
                pair = uT[:, bass.ds(p * KD * 2 * P, KD * 2 * P)]
                if isinstance(p, int) and p == 0:
                    act.wait_ge(uT_ready, KD * NP)
                a.activation(pair, pair, ACT.Silu).then_inc(gates_ready, 1)

            def n_hi(p):
                act.wait_ge(n_ready, 2 * (p + 1))
                wait(act, nT_done, p)
                a.activation(n16[:, :, 0:D], n32, ACT.Copy).then_inc(nh_ready, 1)

            def y_norm(p):
                act.wait_ge(nT_done, p + 1)
                wait(act, z_ready, p)
                for c in range(KD):
                    a.activation(yT[:, c, :], ps_c0[:, c * 2 * P:(c + 1) * 2 * P], ACT.Identity,
                                 bias=par[:, 2, c:c + 1], scale=par[:, 1, c:c + 1]).then_inc(yT_ready, 1)

            def z_hi(p):
                act.wait_ge(z_ready, p + 1)
                wait(act, f_done, p)
                a.activation(z16[:, 0, :], z32, ACT.Copy).then_inc(zh_ready, 1)

            def step(p, b):
                t = 4 * p
                silu(t, 0)
                h_hi(t, 0, 2 * p)
                u_gates(p)
                if not (isinstance(p, int) and p == 0):
                    y_out(t - 2, 2, 0, p - 1)
                silu(t + 1, 1)
                n_hi(p)
                h_hi(t + 1, 1, 2 * p)
                if not (isinstance(p, int) and p == 0):
                    y_out(t - 1, 3, 1, p - 1)
                silu(t + 2, 0)
                h_hi(t + 2, 0, 2 * p + 1)
                y_out(t, 0, 0, p)
                y_norm(p)
                silu(t + 3, 1)
                z_hi(p)
                h_hi(t + 3, 1, 2 * p + 1)
                y_out(t + 1, 1, 1, p)
            act.wait_ge(w_lo, E - 1)
            act.wait_ge(kT_done, 16 * (TT // CH))
            for lo, hi, b in loops(step):
                with act.Fori(lo, hi) as p:
                    step(p, b)
            for t in range(4 * NP, ST):
                silu(t, t % 2)
                h_hi(t, t % 2, t // 2)
                y_out(t - 2, (t - 2) % 4, t % 2, (t - 2) // 4)
            for t in range(ST - 2, ST):
                y_out(t, t % 4, t % 2, t // 4)

        @block.vector
        def _(dve):
            v = nc.vector
            v.memset(log_scale[:], math.log(SCALE) - 1.0).then_inc(log_scale_set, 1)

            def rsqrt(y, var, ve, sq, eps, done, call):
                n = [RSQRT_OPS * call]

                def link(instruction):
                    n[0] = n[0] + 1
                    instruction.then_inc(done, 1)
                    dve.wait_ge(done, n[0])
                link(v.tensor_scalar(ve, var, eps, None, ALU.add))
                link(v.tensor_scalar(y.bitcast(I32), ve.bitcast(I32), -0.5, float(0x5f3759df),
                                     ALU.mult, ALU.add))
                for _ in range(NEWTON):
                    link(v.tensor_tensor(sq, y, y, ALU.mult))
                    link(v.scalar_tensor_tensor(sq, sq, -0.5, ve, ALU.mult, ALU.mult))
                    link(v.scalar_tensor_tensor(y, sq, 1.5, y, ALU.add, ALU.mult))

            def norm(t0, n, call):
                for t in range(t0, t0 + n):
                    v.bn_stats(stats[:, t, :], area[:, t * D:(t + 1) * D]).then_inc(st_done, 1)
                for t in range(t0, t0 + n):
                    dve.wait_ge(st_done, t + 1)
                    v.bn_aggr(mv[:, t, :], stats[:, t, :]).then_inc(mv_done, 1)
                dve.wait_ge(mv_done, t0 + n)
                rsqrt(rstd[:, t0:t0 + n], mv[:, t0:t0 + n, 1:2].rearrange("p t a -> p (t a)"),
                      newton[:, 0, t0:t0 + n], newton[:, 1, t0:t0 + n], EPS, rstd_done, call)
                v.scalar_tensor_tensor(shift[:, t0:t0 + n], mv[:, t0:t0 + n, 0:1].rearrange("p t a -> p (t a)"),
                                       -1.0, rstd[:, t0:t0 + n], ALU.mult, ALU.mult).then_inc(shift_ready, 1)

            def rows(t0, n):
                for t in range(t0, t0 + n):
                    v.tensor_scalar(xn32[:, t, :], area[:, t * D:(t + 1) * D], rstd[:, t:t + 1], shift[:, t:t + 1],
                                    ALU.mult, ALU.add).then_inc(xn_ready, 1)

            def attn_part(chunks, c0, c1):
                def cols(u):
                    return u.rearrange("p (k c) -> p k c", c=AC)[:, chunks, c0:c1]
                v.scalar_tensor_tensor(cols(wa16[:, 1, :]), cols(attn32), SCALE, cols(wa16[:, 0, :]),
                                       ALU.mult, ALU.subtract).then_inc(attn_lo, 1)
            dve.wait_ge(x_first, 16)
            norm(0, CH, 0)
            dve.wait_ge(shift_ready, 1)
            rows(0, CH)
            dve.wait_ge(x_rest, 16)
            norm(CH, TT - CH, 1)
            dve.wait_ge(shift_ready, 2)
            rows(CH, TT - CH)
            dve.wait_ge(attn_hi, 1)
            attn_part(slice(0, KD), 0, E)
            for t in range(CH + 1, TT, 2):
                dve.wait_ge(x_turned, t + 1)
                v.tensor_copy(xT[:, t, :, :].rearrange("p c i -> p (c i)"), ps_x[t % CH][:]
                              ).then_inc(xT_dve, 1)
                if (t - CH) // 2 < KD:
                    chunk = (t - CH) // 2
                    attn_part(slice(chunk, chunk + 1), E, AC)

            def expert_lo(e):
                dve.wait_ge(w_hi, e + 1)
                v.scalar_tensor_tensor(w16[:, e, 1, :], regions[:, (e + 2) * WCOLS:(e + 3) * WCOLS], SCALE,
                                       w16[:, e, 0, :], ALU.mult, ALU.subtract).then_inc(w_lo, 1)
            at = [TT * D // 2]

            def tmp(shape):
                n = 1
                for s in shape:
                    n *= s
                at[0] += n
                return view(area, at[0] - n, shape)
            count = [0]

            def chain(instruction):
                count[0] += 1
                instruction.then_inc(route_step, 1)
                dve.wait_ge(route_step, count[0])

            sc2, pick, dest = [tmp([TT, E]) for _ in range(3)]
            hits, part = [tmp([TOPK, TT * E]) for _ in range(2)]
            hit1, hit2 = [hits[:, k, :].rearrange("p (t e) -> p t e", e=E) for k in range(TOPK)]
            first, second, i1, i2, gap, ge1 = [tmp([TT]) for _ in range(6)]
            slotf = tmp([TOPK, TT])
            tiles, base, end, lower, freed = [tmp([E]) for _ in range(5)]
            over = tmp([E, TT])
            sums = tmp([E, E])
            expf = tmp([ST, E - 1])
            expn = tmp([ST])
            padf = tmp([PADS, E])
            padn = tmp([PADS])

            def per_tile(u):
                return u.unsqueeze(2).broadcast_to([P, TT, E])

            def per_expert(u):
                return u.unsqueeze(1).broadcast_to([P, TT, E])
            dve.wait_ge(consts_ready, 1)
            dve.wait_ge(scores_done, TT)
            sc = ps_gate[:, 0:TT * E].rearrange("p (t e) -> p t e", e=E)
            chain(v.tensor_reduce(first, sc, AX.X, ALU.max))
            chain(v.tensor_tensor(hit1, sc, per_tile(first), ALU.is_equal))
            chain(v.tensor_tensor(pick, hit1, per_expert(rev[:]), ALU.mult))
            chain(v.tensor_reduce(i1, pick, AX.X, ALU.max))
            chain(v.tensor_tensor(hit1, per_expert(rev[:]), per_tile(i1), ALU.is_equal))
            chain(v.scalar_tensor_tensor(sc2, hit1, -BIG, sc, ALU.mult, ALU.add))
            chain(v.tensor_reduce(second, sc2, AX.X, ALU.max))
            v.tensor_tensor(gap_in[:], second, first, ALU.subtract).then_inc(gap_ready, 1)
            chain(v.tensor_tensor(hit2, sc2, per_tile(second), ALU.is_equal))
            chain(v.tensor_tensor(pick, hit2, per_expert(rev[:]), ALU.mult))
            chain(v.tensor_reduce(i2, pick, AX.X, ALU.max))
            chain(v.tensor_tensor(hit2, per_expert(rev[:]), per_tile(i2), ALU.is_equal))
            v.tensor_tensor(m16[:], hit1, hit2, ALU.add).then_inc(mask_ready, 1)
            dve.wait_ge(ranks_done, 1)
            total = ps_route[:, TT * E:TT * E + E]
            chain(v.tensor_tensor(over, total.unsqueeze(2).broadcast_to([P, E, TT]),
                                  step128[:].unsqueeze(1).broadcast_to([P, E, TT]), ALU.is_gt))
            chain(v.tensor_reduce(tiles, over, AX.X, ALU.add))
            chain(v.tensor_tensor(sums, before[:], tiles.unsqueeze(1).broadcast_to([P, E, E]), ALU.mult))
            chain(v.tensor_reduce(base, sums, AX.X, ALU.add))
            chain(v.scalar_tensor_tensor(dest, per_expert(base), float(P),
                                         ps_route[:, 0:TT * E].rearrange("p (t e) -> p t e", e=E),
                                         ALU.mult, ALU.add))
            chain(v.tensor_tensor(part, hits, dest.rearrange("p t e -> p (t e)").unsqueeze(1).broadcast_to(
                [P, TOPK, TT * E]), ALU.mult))
            chain(v.tensor_reduce(slotf.rearrange("p k t -> p (k t)"),
                                  part.rearrange("p k (t e) -> p (k t) e", e=E), AX.X, ALU.add))
            v.tensor_copy(slot[:], slotf).then_inc(slot_ready, 1)
            dve.wait_ge(gexp_ready, 1)
            chain(v.tensor_scalar(ge1, gate2[:], SCALE, SCALE, ALU.mult, ALU.add))
            chain(v.reciprocal(gap, ge1))
            v.tensor_copy(xrow[:, :, D + 1:D + 2], gap.unsqueeze(2)).then_inc(gate_ready, 1)
            v.tensor_tensor(gate2[:], gate2[:], gap, ALU.mult).then_inc(gate_ready, 1)
            chain(v.tensor_tensor(sums, before[:], total.unsqueeze(1).broadcast_to([P, E, E]), ALU.mult))
            chain(v.tensor_reduce(lower, sums, AX.X, ALU.add))
            chain(v.scalar_tensor_tensor(freed, base, float(P), lower, ALU.mult, ALU.subtract))
            chain(v.tensor_tensor(padf, pad_no[:].unsqueeze(2).broadcast_to([P, PADS, E]),
                                  freed.unsqueeze(1).broadcast_to([P, PADS, E]), ALU.is_ge))
            chain(v.tensor_tensor(padf, padf, total.unsqueeze(1).broadcast_to([P, PADS, E]), ALU.mult))
            chain(v.tensor_reduce(padn, padf, AX.X, ALU.add))
            v.tensor_tensor(padslot[:], padn, pad_no[:], ALU.add).then_inc(slot_ready, 1)
            chain(v.tensor_tensor(end, base, tiles, ALU.add))
            chain(v.tensor_tensor(expf, end[:, 0:E - 1].unsqueeze(1).broadcast_to([P, ST, E - 1]),
                                  tile_no[:].unsqueeze(2).broadcast_to([P, ST, E - 1]), ALU.is_le))
            chain(v.tensor_reduce(expn, expf, AX.X, ALU.add))
            v.tensor_copy(tile_expert[:], expn).then_inc(slot_ready, 1)

            def kv_maps(i):
                for r in range(CH):
                    t = CH * i + r
                    dve.wait_ge(exps_ready, 2 * (t + 1))
                    v.scalar_tensor_tensor(kv32[r][:, 0:D], kv32[r][:, 0:D], SCALE, ps_qv[r][:, 0:D],
                                           ALU.min, ALU.max).then_inc(kv32_ready, 1)
                    v.scalar_tensor_tensor(kv32[r][:, D:2 * D], kv32[r][:, D:2 * D], 1.0,
                                           ps_qv[r][:, D:2 * D], ALU.add, ALU.mult).then_inc(kv32_ready, 1)

            def k_lo(i):
                for r in range(CH):
                    t = CH * i + r
                    dve.wait_ge(kh_ready, 2 * (t + 1))
                    v.tensor_tensor(krow[:, r, D:2 * D], kv32[r][:, 0:D], krow[:, r, 0:D],
                                    ALU.subtract).then_inc(kl_ready, 1)

            def kv_blocks(b):
                dve.wait_ge(kv_mm, TB * (b + 1))
                if b > 0:
                    dve.wait_ge(kv_ready, b)
                for c in range(KD):
                    v.tensor_tensor(kvm[:, c, :], ps_kv[c][:, 0:P], kv_mask[:], ALU.mult
                                    ).then_inc(kvm_ready, 1)

            def kv_lo(b):
                dve.wait_ge(kv_hi, b + 1)
                v.tensor_tensor(kv16[:, b, 1, :], kvm[:, :, :].rearrange("p c d -> p (c d)"),
                                kv16[:, b, 0, :], ALU.subtract).then_inc(kv_ready, 1)

            kv_maps(0)
            expert_lo(1)
            k_lo(0)
            expert_lo(2)
            kv_maps(1)
            expert_lo(3)
            k_lo(1)
            expert_lo(4)
            kv_maps(2)
            kv_blocks(0)
            expert_lo(5)
            k_lo(2)
            kv_lo(0)
            expert_lo(6)
            kv_maps(3)
            expert_lo(7)
            k_lo(3)
            kv_blocks(1)
            kv_lo(1)

            def h_mul(t, r2):
                dve.wait_ge(b_done, t + 1)
                dve.wait_ge(s_ready, t + 1)
                wait(dve, hh_ready, t - 1)
                v.scalar_tensor_tensor(h32[r2], ps_b[r2][:], 1.0 / SCALE, s32[r2],
                                       ALU.mult, ALU.mult).then_inc(h_ready, 1)

            def h_lo(t, r2):
                dve.wait_ge(hh_ready, t + 1)
                v.tensor_tensor(h16[r2][:, 1, :], h32[r2], h16[r2][:, 0, :], ALU.subtract
                                ).then_inc(hl_ready, 1)

            def center(p):
                dve.wait_ge(o_done, p + 1)
                for j in range(2):
                    v.bn_stats(stats2[:, j, :], ps_c1[:, j * D:(j + 1) * D]).then_inc(c_stats, 1)
                for j in range(2):
                    hold(dve, c_stats, 2 * p + j + 1)
                    v.bn_aggr(mv2[:, j, :], stats2[:, j, :]).then_inc(c_mv, 1)
                dve.wait_ge(c_mv, 2 * p + 2)
                rsqrt(rstd2, mv2[:, :, 1:2].rearrange("p t a -> p (t a)"), newton[:, 0, 0:2],
                      newton[:, 1, 0:2], EPS, c_rstd, p)
                for j in range(2):
                    v.tensor_scalar(n32[:, j, :], ps_c1[:, j * D:(j + 1) * D], mv2[:, j, 0:1],
                                    rstd2[:, j:j + 1], ALU.subtract, ALU.mult).then_inc(n_ready, 1)

            def n_lo(p):
                dve.wait_ge(nh_ready, p + 1)
                v.tensor_tensor(n16[:, :, D:2 * D], n32, n16[:, :, 0:D], ALU.subtract
                                ).then_inc(nl_ready, 1)

            def z_mul(p):
                dve.wait_ge(yT_ready, 2 * (p + 1))
                dve.wait_ge(gates_ready, p + 1)
                v.tensor_tensor(z32, yT[:, :, :].rearrange("p c t -> p (c t)"),
                                uT[:, bass.ds(p * KD * 2 * P, KD * 2 * P)], ALU.mult).then_inc(z_ready, 1)

            def z_lo(p):
                dve.wait_ge(zh_ready, p + 1)
                v.tensor_tensor(z16[:, 1, :], z32, z16[:, 0, :], ALU.subtract).then_inc(zl_ready, 1)

            def finish(p):
                dve.wait_ge(f_done, p + 1)
                wait(dve, fin_added, 16 * p)
                v.scalar_tensor_tensor(fin, ps_c1[:, :].rearrange("p (j d) -> p j d", d=D), 1.0 / SCALE,
                                       o_bias[:].unsqueeze(1).broadcast_to([P, 2, D]),
                                       ALU.mult, ALU.add).then_inc(fin_ready, 1)

            def step(p, b):
                t = 4 * p
                h_mul(t, 0)
                h_lo(t, 0)
                center(p)
                h_mul(t + 1, 1)
                h_lo(t + 1, 1)
                n_lo(p)
                h_mul(t + 2, 0)
                h_lo(t + 2, 0)
                z_mul(p)
                h_mul(t + 3, 1)
                z_lo(p)
                h_lo(t + 3, 1)
                finish(p)
            dve.wait_ge(w_lo, E - 1)
            dve.wait_ge(kT_done, 16 * (TT // CH))
            for lo, hi, b in loops(step):
                with dve.Fori(lo, hi) as p:
                    step(p, b)
            for t in range(4 * NP, ST):
                h_mul(t, t % 2)
                h_lo(t, t % 2)

        @block.tensor
        def _(pe):
            mm = nc.tensor.matmul
            PASSES = ((0, 0), (0, 1), (1, 0))

            def turn_x(t):
                pe.wait_ge(xl_ready, t + 1)
                if t >= CH:
                    wait_xT(t - CH)
                for c in range(2 * KD):
                    last = mm(ps_x[t % CH][:, c * P:(c + 1) * P], xrow16[:, t, c * P:(c + 1) * P], ident[:],
                              start=True, stop=True)
                last.then_inc(x_turned, 1)

            def wait_xT(t):
                if t > CH and t % 2 == 1:
                    pe.wait_ge(xT_dve, (t - CH + 1) // 2)
                else:
                    pe.wait_ge(xT_act, t + 1 if t < CH else CH + (t - CH) // 2 + 1)

            def score(t):
                wait_xT(t)
                for k in range(KD):
                    for n, (w, d) in enumerate(PASSES):
                        last = mm(ps_gate[:, t * E:(t + 1) * E], xT[:, t, KD * d + k, :],
                                  wa16[:, w, k * AC + GATE:k * AC + GATE + E],
                                  start=(k == 0 and n == 0), stop=(k == KD - 1 and n == 2))
                last.then_inc(scores_done, 1)
            pe.wait_ge(consts_ready, 1)
            for t in range(TT):
                turn_x(t)
                if t == CH + 2:
                    pe.wait_ge(attn_lo, 1)
                if t >= CH + 2:
                    score(t - CH - 2)
            for t in range(TT - CH - 2, TT):
                score(t)

            def qv(t):
                r = t % CH
                wait(pe, kv32_ready, 2 * (t + 1 - CH))
                mm(ps_qv[r][:], ones[0:2, :], qv_bias16[:], start=True, stop=False)
                for k in range(KD):
                    for n, (w, d) in enumerate(PASSES):
                        last = mm(ps_qv[r][:], xT[:, t, KD * d + k, :],
                                  wa16[:, w, k * AC + WQ:k * AC + WQ + 2 * D],
                                  start=False, stop=(k == KD - 1 and n == 2))
                last.then_inc(qv_done, 1)
            pe.wait_ge(attn_lo, 1 + KD)
            pe.wait_ge(bias_lo, 2)
            qv(0)

            pe.wait_ge(mask_ready, 1)
            mm(ps_route[:, 0:TT * E], strict[:], m16[:, :, :].rearrange("p t e -> p (t e)"),
               start=True, stop=False)
            for s in range(1, TT):
                mm(ps_route[:, s * E:TT * E], ones[:], m16[:, 0:TT - s, :].rearrange("p t e -> p (t e)"),
                   start=False, stop=(s == TT - 1))
            for s in range(TT):
                last = mm(ps_route[:, TT * E:TT * E + E], ones[:], m16[:, s, :],
                          start=(s == 0), stop=(s == TT - 1))
            last.then_inc(ranks_done, 1)

            def kv(t):
                r = t % CH
                start, stop = t % TB == 0, t % TB == TB - 1
                pe.wait_ge(kh_ready, 2 * (t + 1))
                pe.wait_ge(kv32_ready, 2 * (t + 1))
                if t == TB:
                    pe.wait_ge(kvm_ready, KD)
                for c in range(KD):
                    last = mm(ps_kv[c][:, 0:P], kv32[r][:, c * P:(c + 1) * P],
                              kv32[r][:, D + c * P:D + (c + 1) * P], start=start, stop=stop,
                              skip_group_check=True)
                last.then_inc(kv_mm, 1)
            for t in range(1, CH):
                qv(t)

            def u_proj(p):
                if p == 0:
                    pe.wait_ge(slot_ready, 3)
                if p >= 2:
                    pe.wait_ge(uT_ready, 2 * (p - 1))
                for c in range(KD):
                    for k in range(KD):
                        at = k * AC + WU + c * P
                        for n, (w, d) in enumerate(PASSES):
                            last = mm(ps_u[p % 2][:, c * 2 * P:(c + 1) * 2 * P].rearrange("p (j i) -> p j i", j=2),
                                      wa16[:, w, at:at + P], xT[:, 2 * p:2 * p + 2, KD * d + k, :],
                                      start=(k == 0 and n == 0), stop=(k == KD - 1 and n == 2))
                last.then_inc(u_done, 1)
            for g in range(TT // CH):
                for t in range(CH * g, CH * (g + 1)):
                    if t + CH < TT:
                        qv(t + CH)
                    kv(t)
                u_proj(2 * g)
                u_proj(2 * g + 1)

            def expert_of(t):
                return pe.value_load(tile_expert[0:1, bass.ds(t, 1)], min_val=0, max_val=E - 1)

            def hidden(t, r, r2, visit):
                e = expert_of(t)
                pe.wait_ge(xg_loaded[r], 16 * (visit + 1))
                for bank_, col, done, taken in ((ps_a[r2], W1, a_done, s_ready), (ps_b[r2], W3, b_done, h_ready)):
                    wait(pe, taken, t - 1)
                    for k in range(KD):
                        at = col + k * I
                        for n, (w, d) in enumerate(PASSES):
                            last = mm(bank_[:], xg[r][:, KD * d + k, :],
                                      w16[:, bass.ds(e, 1), w, at:at + I].rearrange("p a c -> p (a c)"),
                                      start=(k == 0 and n == 0), stop=(k == KD - 1 and n == 2))
                    last.then_inc(done, 1)

            def down(t, r2, visit2):
                e = expert_of(t)
                pe.wait_ge(hT_done[r2], 16 * (visit2 + 1))
                wait(pe, y_ready, t - 1)
                for c in range(IC):
                    at = W2 + c * D
                    for n, (w, d) in enumerate(PASSES):
                        last = mm(ps_y[r2][:, 0:D], hT[r2][:, IC * d + c, :],
                                  w16[:, bass.ds(e, 1), w, at:at + D].rearrange("p a c -> p (a c)"),
                                  start=(c == 0 and n == 0), stop=(c == IC - 1 and n == 2))
                last.then_inc(y_done, 1)

            def q_kv(p, b):
                wait(pe, fin_ready, p)
                for j in range(2):
                    for c in range(KD):
                        for n, (w, d) in enumerate(PASSES):
                            last = mm(ps_c1[:, j * D + c * P:j * D + (c + 1) * P],
                                      kT[:, bass.ds(2 * p + j, 1), KD * d + c, :].rearrange("p a i -> p (a i)"),
                                      kv16[:, b, w, c * P:(c + 1) * P],
                                      start=(n == 0), stop=(n == 2))
                last.then_inc(o_done, 1)

            def turn(p):
                pe.wait_ge(nl_ready, p + 1)
                wait(pe, yT_ready, 2 * p)
                for c in range(KD):
                    for j in range(2):
                        for w in range(2):
                            last = mm(ps_c0[:, c * 2 * P + j * P:c * 2 * P + (j + 1) * P],
                                      n16[:, j, w * D + c * P:w * D + (c + 1) * P], ident[:],
                                      start=(w == 0), stop=(w == 1))
                last.then_inc(nT_done, 1)

            def project(p):
                pe.wait_ge(zl_ready, p + 1)
                for j in range(2):
                    for c in range(KD):
                        at = c * AC + WO
                        for n, (w, d) in enumerate(PASSES):
                            last = mm(ps_c1[:, j * D:(j + 1) * D],
                                      z16[:, d, c * 2 * P + j * P:c * 2 * P + (j + 1) * P],
                                      wa16[:, w, at:at + D],
                                      start=(c == 0 and n == 0), stop=(c == KD - 1 and n == 2))
                last.then_inc(f_done, 1)

            def step(p, b):
                t = 4 * p
                rest = not (isinstance(p, int) and p == 0)
                hidden(t, 0, 0, p)
                if rest:
                    down(t - 2, 0, 2 * p - 1)
                else:
                    pe.wait_ge(kT_done, 16 * (TT // CH))
                    pe.wait_ge(kv_ready, BATCHES)
                q_kv(p, b)
                hidden(t + 1, 1, 1, p)
                if rest:
                    down(t - 1, 1, 2 * p - 1)
                hidden(t + 2, 2, 0, p)
                down(t, 0, 2 * p)
                if rest:
                    turn(p)
                hidden(t + 3, 3, 1, p)
                if not rest:
                    turn(p)
                down(t + 1, 1, 2 * p)
                project(p)
            pe.wait_ge(slot_ready, 3)
            pe.wait_ge(w_lo_pool, 2)
            pe.wait_ge(w_lo, E - 1)
            pe.wait_ge(uT_ready, 2 * NP)
            for lo, hi, b in loops(step):
                with pe.Fori(lo, hi) as p:
                    step(p, b)
            for t in range(4 * NP, ST):
                hidden(t, t % 4, t % 2, t // 4)
                down(t - 2, t % 2, (t - 2) // 2)
            for t in range(ST - 2, ST):
                down(t, t % 2, t // 2)


def kernel(**inputs):
    import numpy as np
    import concourse.bacc as bacc
    from concourse.bass_utils import run_bass_kernel_spmd

    def get(name):
        return np.ascontiguousarray(inputs["L0_" + name])

    x = get("attn_x")
    shape = x.shape
    rows = [get("ffn_gate_w").T, get("attn_Wu"), get("attn_Wqk"), get("attn_Wv"), get("attn_Wo")]
    wattn = np.concatenate(rows, axis=1).reshape(KD, P, AC).transpose(1, 0, 2).reshape(P, KD * AC)

    def chunks(w):
        e, k, m = w.shape
        return w.reshape(e, k // P, P, m).transpose(0, 2, 1, 3).reshape(e, P, k // P * m)
    wexp = np.concatenate([chunks(get("ffn_w1").transpose(0, 2, 1)), chunks(get("ffn_w3").transpose(0, 2, 1)),
                           chunks(get("ffn_w2").transpose(0, 2, 1))], axis=2)
    params = np.stack([get(n).reshape(KD, P).T for n in ("attn_bu", "attn_ln_g", "attn_ln_b")], axis=1)
    bias_rows = np.concatenate([get("attn_bqk"), get("attn_bv"), get("attn_bo")])
    arrays = {"x": x.reshape(TOKENS, D), "wattn": wattn, "wexp": wexp, "params": params,
              "bias_rows": bias_rows}
    arrays = {n: np.ascontiguousarray(a) for n, a in arrays.items()}

    nc = bacc.Bacc("TRN2", target_bir_lowering=False, num_devices=1)
    args = [nc.dram_tensor(n, a.shape, mybir.dt.from_np(a.dtype), kind="ExternalInput").ap()
            for n, a in arrays.items()]
    out = nc.dram_tensor("out", (TOKENS + P, D), F32, kind="ExternalOutput").ap()
    build(nc, *args, out)
    r = run_bass_kernel_spmd(nc, [arrays], core_ids=[0])
    return r.results[0]["out"][0:TOKENS].reshape(shape)
```
